# Optimizing a Trainium2 kernel written in Bass

```python
import numpy as np
import jax
import jax.numpy as jnp

def _softmax(x, axis=-1):
    return jax.nn.softmax(x, axis=axis)
def _gelu(x):
    return jax.nn.gelu(x, approximate=True)
def _silu(x):
    return jax.nn.silu(x)
def _sigmoid(x):
    return jax.nn.sigmoid(x)
def _layernorm(x, axis=-1, eps=1e-5):
    m = jnp.mean(x, axis=axis, keepdims=True)
    v = jnp.var(x, axis=axis, keepdims=True)
    return (x - m) / jnp.sqrt(v + eps)
def _scatter_add(tgt, idx, src, axis=0):
    return tgt.at[idx].add(src)
def _segment_sum(src, seg, n):
    return jax.ops.segment_sum(src, seg, n)

kernel_name = 'mk_conv_seq_d1_conv_nchw512_b19259'

def setup_inputs(seed: int = 0):
    np.random.seed(seed)
    _w = jnp.asarray
    def _rec_inputs():
        import jax
        import jax.numpy as jnp
        _gk = jax.random.key(seed)
        x = 7.22e-05 + 1 * jax.random.normal(jax.random.fold_in(_gk, 1), (16, 512, 32, 32), jnp.float32)
        return x
    x = _rec_inputs()
    def _L0_conv_setup():
        import jax, jax.numpy as jnp
        import numpy as np
        C = 512
        NUM_HEADS = 8
        HEAD_DIM = C // NUM_HEADS
        GROUPS = 32
        EPS = 1e-05

        def _group_norm(x, w, b):
            N, Cc, H, W = x.shape
            xg = x.reshape(N, GROUPS, Cc // GROUPS, H, W)
            mean = xg.mean(axis=(2, 3, 4), keepdims=True)
            var = xg.var(axis=(2, 3, 4), keepdims=True)
            xg = (xg - mean) * jax.lax.rsqrt(var + EPS)
            return xg.reshape(N, Cc, H, W) * w[None, :, None, None] + b[None, :, None, None]
        key = jax.random.key(seed)
        ks = jax.random.split(key, 7)
        N, H, W = (16, 32, 32)
        x = jax.random.normal(ks[0], (N, C, H, W), dtype=jnp.float32)
        norm_w = jax.random.normal(ks[1], (C,), dtype=jnp.float32) * 0.02 + 1.0
        norm_b = jax.random.normal(ks[2], (C,), dtype=jnp.float32) * 0.02
        qkv_w = jax.random.normal(ks[3], (3 * C, C), dtype=jnp.float32) * (1.0 / np.sqrt(C))
        qkv_b = jax.random.normal(ks[4], (3 * C,), dtype=jnp.float32) * 0.02
        proj_w = jax.random.normal(ks[5], (C, C), dtype=jnp.float32) * (1.0 / np.sqrt(C))
        proj_b = jax.random.normal(ks[6], (C,), dtype=jnp.float32) * 0.02
        return {'x': x, 'norm_w': norm_w, 'norm_b': norm_b, 'qkv_w': qkv_w, 'qkv_b': qkv_b, 'proj_w': proj_w, 'proj_b': proj_b}
    _L0_conv_all = _L0_conv_setup()
    _L0_conv_in = {k: v for k, v in _L0_conv_all.items() if k in ('norm_w', 'norm_b', 'qkv_w', 'qkv_b', 'proj_w', 'proj_b', )}
    del _L0_conv_all

    return {
        "x": x,
        "L0_conv_norm_w": _L0_conv_in["norm_w"],
        "L0_conv_norm_b": _L0_conv_in["norm_b"],
        "L0_conv_qkv_w": _L0_conv_in["qkv_w"],
        "L0_conv_qkv_b": _L0_conv_in["qkv_b"],
        "L0_conv_proj_w": _L0_conv_in["proj_w"],
        "L0_conv_proj_b": _L0_conv_in["proj_b"],
    }

def reference(x, L0_conv_norm_w, L0_conv_norm_b, L0_conv_qkv_w, L0_conv_qkv_b, L0_conv_proj_w, L0_conv_proj_b):
    import jax
    import jax.numpy as jnp
    def _L0_conv_ref(x, norm_w, norm_b, qkv_w, qkv_b, proj_w, proj_b):
        import jax, jax.numpy as jnp
        import numpy as np
        C = 512
        NUM_HEADS = 8
        HEAD_DIM = C // NUM_HEADS
        GROUPS = 32
        EPS = 1e-05

        def _group_norm(x, w, b):
            N, Cc, H, W = x.shape
            xg = x.reshape(N, GROUPS, Cc // GROUPS, H, W)
            mean = xg.mean(axis=(2, 3, 4), keepdims=True)
            var = xg.var(axis=(2, 3, 4), keepdims=True)
            xg = (xg - mean) * jax.lax.rsqrt(var + EPS)
            return xg.reshape(N, Cc, H, W) * w[None, :, None, None] + b[None, :, None, None]
        N, Cc, H, W = x.shape
        S = H * W
        h = _group_norm(x, norm_w, norm_b)
        qkv = jnp.einsum('nchw,oc->nohw', h, qkv_w) + qkv_b[None, :, None, None]
        q, k, v = jnp.split(qkv, 3, axis=1)
        q = q.reshape(N, NUM_HEADS, HEAD_DIM, S)
        k = k.reshape(N, NUM_HEADS, HEAD_DIM, S)
        v = v.reshape(N, NUM_HEADS, HEAD_DIM, S)
        scale = HEAD_DIM ** (-0.5)
        attn = jnp.einsum('nhds,nhdt->nhst', q, k) * scale
        attn = jax.nn.softmax(attn, axis=-1)
        out = jnp.einsum('nhst,nhdt->nhds', attn, v)
        out = out.reshape(N, Cc, H, W)
        out = jnp.einsum('nchw,oc->nohw', out, proj_w) + proj_b[None, :, None, None]
        return out + x

    def _gn(v, G=32, eps=1e-5):
        B_, C_, H_, W_ = v.shape
        g = v.reshape(B_, G, C_ // G, H_, W_)
        m = jnp.mean(g, axis=(2, 3, 4), keepdims=True)
        s = jnp.var(g, axis=(2, 3, 4), keepdims=True)
        return ((g - m) / jnp.sqrt(s + eps)).reshape(v.shape)

    def _ln_c(v, eps=1e-6):
        m = jnp.mean(v, axis=1, keepdims=True)
        s = jnp.var(v, axis=1, keepdims=True)
        return (v - m) / jnp.sqrt(s + eps)

    def _ln_t(v, eps=1e-5):
        m = jnp.mean(v, axis=-1, keepdims=True)
        s = jnp.var(v, axis=-1, keepdims=True)
        return (v - m) / jnp.sqrt(s + eps)

    def _to_tokens(v):
        B_, C_, H_, W_ = v.shape
        return v.reshape(B_, C_, H_ * W_).transpose(0, 2, 1)
    def _from_tokens(t, like):
        B_, C_, H_, W_ = like.shape
        return t.transpose(0, 2, 1).reshape(B_, C_, H_, W_)

    x = _L0_conv_ref(x, L0_conv_norm_w, L0_conv_norm_b, L0_conv_qkv_w, L0_conv_qkv_b, L0_conv_proj_w, L0_conv_proj_b)
    return x


_drawn_inputs = setup_inputs


def setup_inputs(seed=0):
    import zlib

    import numpy as np

    out = dict(_drawn_inputs(seed))
    spreads = {}
    factors = {'L0_conv_norm_w': 8.0,
     'L0_conv_qkv_b': 2.894,
     'L0_conv_proj_b': 21.776,
     'L0_conv_norm_b': 2.891}
    for name, (base, spread) in spreads.items():
        noise = np.random.default_rng([zlib.crc32(name.encode()), seed]).standard_normal(out[name].shape)
        drawn = base * np.exp(spread * noise) if base else spread * noise
        out[name] = jnp.asarray(drawn.astype(out[name].dtype))
    for name, factor in factors.items():
        out[name] = (out[name] * factor).astype(out[name].dtype)
    return out
```

```python
from contextlib import ExitStack

import concourse.bass as bass
from concourse import mybir

N_IMG, C, S = 16, 512, 1024
HEADS, D = 8, 64
P128 = 128
KT = C // P128
PAIRS = HEADS // 2
ST = S // P128
TILES = 2 * ST
GRP = 8
GW = 256
HALF = 512
EPS = 1e-5
SCALE = D ** -0.5
CHUNKS = 6
PROJ = 2 * KT
RES = 4
WRING = 4
LAST = N_IMG - 1

QKV_SLOTS = [[1, 2, 3, 4, 5, 6], [1, 3, 5, 7, 9, 11], [1, 2, 3, 4, 5, 6], [2, 4, 6, 8, 10, 12]]
VT_SLOT = [11, 13, 8, 14]
PROJ_SLOTS = [7, 8, 9, 10, 12, 13, 14, 15]
STAT_SLOTS = [0, 2, 4, 6]
GN_MEAN_SLOT, GN_VAR_SLOT = 8, 10
NORM_SLOTS = [7, 9, 11, 13]


def qkv_chunk_at(p, slot, has_next):
    if p == PAIRS - 1 and not has_next:
        return None
    return QKV_SLOTS[p].index(slot) if slot in QKV_SLOTS[p] else None


def proj_chunk_at(p, slot, has_prev):
    return PROJ_SLOTS.index(slot) if p == 0 and has_prev and slot in PROJ_SLOTS else None


def vt_at(p, slot, has_next):
    return slot == VT_SLOT[p] and (p < PAIRS - 1 or has_next)


def block_list(has_prev, has_next):
    out = []
    for p in range(PAIRS):
        if p < PAIRS - 1 or has_next:
            out += [("qkv", p + 1, t) for t in range(3)]
        if p == 0 and has_prev:
            out += [("proj", m) for m in range(KT)]
    return out


def block_use(n, local):
    if isinstance(n, int) and n == 0:
        u = 3 + local
        return u % WRING, u // WRING + 1
    return (local - 1) % WRING, n * 4 + ((local - 1) // WRING + 1)


def build(nc, x, wqkvT, bqkv, wpT, bp, gnw, gnb, ident_in, avg_in, out):
    fp32, f32r = mybir.dt.float32, mybir.dt.float32r
    ACT = mybir.ActivationFunctionType
    ALU = mybir.AluOpType
    AX = mybir.AxisListType.X

    w_scr = nc.dram_tensor("w_scr", [3 * PAIRS + KT, P128, 2 * KT * P128], fp32, kind="Internal").ap()
    r_scr = nc.dram_tensor("r_scr", [2, 2, S], fp32, kind="Internal").ap()

    with ExitStack() as ctx:
        def sb(name, shape, dt=fp32):
            return ctx.enter_context(nc.sbuf_tensor(name, shape, dt))

        def sem(name):
            return ctx.enter_context(nc.semaphore(name))

        h_hi = sb("h_hi", [P128, KT, S], f32r)
        h_lo = sb("h_lo", [P128, KT, S], f32r)
        w_ring = sb("w_ring", [P128, WRING, 2, KT, P128], f32r)
        Q = sb("Q", [P128, 2, 2, S], f32r)
        K = sb("K", [P128, 2, 2, 2, S], f32r)
        V = sb("V", [P128, 2, ST, 2, 2 * D], f32r)
        pt_hi = sb("pt_hi", [P128, 2, ST, GW], f32r)
        pt_lo = sb("pt_lo", [P128, 2, ST, GW], f32r)
        prob = sb("prob", [P128, 2, S])
        a_hi = sb("a_hi", [P128, KT, S], f32r)
        a_lo = sb("a_lo", [P128, KT, S], f32r)
        x_t = sb("x_t", [P128, 2, S])
        U = sb("U", [P128, 2, S])
        R = sb("R", [P128, S])
        v32 = sb("v32", [P128, S])
        o_tmp = sb("o_tmp", [P128, GW])
        res = sb("res", [P128, RES, HALF])
        ident = sb("ident", [P128, P128])
        avg = sb("avg", [P128, P128])
        b_qkv = sb("b_qkv", [P128, 3 * PAIRS])
        b_p = sb("b_p", [P128, KT])
        gn_w = sb("gn_w", [P128, KT])
        gn_b = sb("gn_b", [P128, KT])
        nmax = sb("nmax", [P128, 2])
        rsum = sb("rsum", [P128, 2, TILES])
        rcp = sb("rcp", [P128, TILES])
        rT = sb("rT", [TILES, P128])
        bn6 = sb("bn6", [P128, KT, 2, 6])
        gsum = sb("gsum", [P128, KT])
        gdev4 = sb("gdev4", [P128, KT, 4])
        gmean = sb("gmean", [P128, KT])
        gdev = sb("gdev", [P128, KT])
        gvar = sb("gvar", [P128, KT])
        grs = sb("grs", [P128, KT])
        m_half = sb("m_half", [P128, KT])
        gn_a = sb("gn_a", [P128, KT])
        gn_c = sb("gn_c", [P128, KT])

        ps_s = ctx.enter_context(nc.psum_tensor("ps_s", [P128, 2, S], fp32))
        ps_t = ctx.enter_context(nc.psum_tensor("ps_t", [P128, S], fp32))
        ps_o = ctx.enter_context(nc.psum_tensor("ps_o", [P128, HALF], fp32))
        ps_f = ctx.enter_context(nc.psum_tensor("ps_f", [P128, HALF], fp32))

        scores_done = sem("scores_done")
        ptrans_done = sem("ptrans_done")
        pv_done = sem("pv_done")
        qkv_done = sem("qkv_done")
        vtrans_done = sem("vtrans_done")
        proj_done = sem("proj_done")
        rtrans_done = sem("rtrans_done")
        gavg_done = sem("gavg_done")
        exp_done = sem("exp_done")
        pt_hi_done = sem("pt_hi_done")
        qkv_hi_done = sem("qkv_hi_done")
        v_hi_done = sem("v_hi_done")
        o_copy_done = sem("o_copy_done")
        a_hi_done = sem("a_hi_done")
        h_hi_done = sem("h_hi_done")
        w_hi_done = sem("w_hi_done")
        max_done = sem("max_done")
        pt_lo_done = sem("pt_lo_done")
        qk_lo_done = sem("qk_lo_done")
        v_lo_done = sem("v_lo_done")
        o_add_done = sem("o_add_done")
        rcp_done = sem("rcp_done")
        rcopy_done = sem("rcopy_done")
        stat_done = sem("stat_done")
        gn_done = sem("gn_done")
        h32_done = sem("h32_done")
        res_done = sem("res_done")
        w_lo_done = sem("w_lo_done")
        bias_done = sem("bias_done")
        dve_step = sem("dve_step")
        root_done = sem("root_done")
        mul_done = sem("mul_done")
        a_lo_done = sem("a_lo_done")
        h_lo_done = sem("h_lo_done")
        half_set = sem("half_set")
        const_in = sem("const_in")
        w_raw_in = [sem(f"w_raw_in{i}") for i in range(4)]
        w_stored = [sem(f"w_stored{i}") for i in range(WRING)]
        w_in = [sem(f"w_in{i}") for i in range(WRING)]
        k_copied = sem("k_copied")
        x_in = [sem(f"x_in{i}") for i in range(2)]
        r_out = sem("r_out")
        r_in = sem("r_in")
        res_in = [sem(f"res_in{i}") for i in range(RES)]
        res_out = [sem(f"res_out{i}") for i in range(RES)]

        block = ctx.enter_context(nc.Block())

        def over_images(eng, body):
            body(0, False, True)
            with eng.Fori(1, LAST) as n:
                body(n, True, True)
            body(LAST, True, False)

        def w_block(kind):
            return 3 * (kind[1] % PAIRS) + kind[2] if kind[0] == "qkv" else 3 * PAIRS + kind[1]

        def block_freed(eng, n, kind):
            if kind[0] == "qkv":
                eng.wait_ge(qkv_done, (n * PAIRS + kind[1]) * CHUNKS + 2 * (kind[2] + 1))
            else:
                eng.wait_ge(proj_done, (n - 1) * PROJ + 2 * (kind[1] + 1))

        @block.sync
        def _(sp):
            sp.dma_start(ident[:], ident_in).then_inc(const_in, 16)
            sp.dma_start(avg[:], avg_in).then_inc(const_in, 16)
            sp.dma_start(b_qkv[:], bqkv).then_inc(const_in, 16)
            sp.dma_start(b_p[:], bp).then_inc(const_in, 16)
            sp.dma_start(gn_w[:], gnw).then_inc(const_in, 16)
            sp.dma_start(gn_b[:], gnb).then_inc(const_in, 16)

            def load_x(m, use):
                k, s = use % KT, use % 2
                if use in (0, 1):
                    if not (isinstance(m, int) and m == 0):
                        sp.wait_ge(h_lo_done, KT * m - 1 + use)
                elif use < 6:
                    sp.wait_ge(stat_done, KT * m + use - 1)
                else:
                    sp.wait_ge(h_lo_done, KT * m + use - 5)
                sp.dma_start(x_t[:, s, :], x[m, k * P128:(k + 1) * P128, :]).then_inc(x_in[s], 16)

            def load_w_raw(b):
                p, t = b // 3, b % 3
                if b < 3 * PAIRS:
                    src = wqkvT[:, t * C + p * P128:t * C + (p + 1) * P128]
                else:
                    m = b - 3 * PAIRS
                    src = wpT[:, m * P128:(m + 1) * P128]
                if b >= 4:
                    sp.wait_ge(w_lo_done, b - 3)
                dst = prob[:, (b % 4) // 2, (b % 2) * HALF:(b % 2 + 1) * HALF]
                sp.dma_start(dst.rearrange("p (k o) -> p k o", k=KT),
                             src.rearrange("(k p) o -> p k o", p=P128)).then_inc(w_raw_in[b % 4], 16)

            def store_w(b):
                sp.wait_ge(w_hi_done, b + 1)
                sp.wait_ge(w_lo_done, b + 1)
                sp.dma_start(w_scr[b], w_ring[:, b % WRING].rearrange("p a k o -> p (a k o)").bitcast(fp32)).then_inc(w_stored[b % WRING], 16)

            def load_w(b, slot):
                sp.dma_start(w_ring[:, slot].rearrange("p a k o -> p (a k o)").bitcast(fp32), w_scr[b]).then_inc(w_in[slot], 16)

            def copy_k(P, par, half):
                sp.wait_ge(qk_lo_done, P * 4 + 3 + half)
                cols = slice(half * HALF, (half + 1) * HALF)
                sp.dma_start(K[D:P128, par, 0, :, cols].bitcast(fp32), K[0:D, par, 0, :, cols].bitcast(fp32)).then_inc(k_copied, 16)
                sp.dma_start(K[0:D, par, 1, :, cols].bitcast(fp32), K[D:P128, par, 1, :, cols].bitcast(fp32)).then_inc(k_copied, 16)

            def spread_r(P, par):
                sp.wait_ge(rcopy_done, P + 1)
                sp.dma_start(r_scr[par].rearrange("h (t s) -> (h t) s", s=P128), rT[:]).then_inc(r_out, 16)
                sp.wait_ge(r_out, (P + 1) * 16)
                if not (isinstance(P, int) and P == 0):
                    sp.wait_ge(mul_done, P)
                sp.dma_start(R[0:D, :], r_scr[par, 0:1, :].broadcast_to((D, S))).then_inc(r_in, 16)
                sp.dma_start(R[D:P128, :], r_scr[par, 1:2, :].broadcast_to((D, S))).then_inc(r_in, 16)

            def res_use(m, c):
                return c % RES, m * (PROJ // RES) + c // RES + 1

            def load_res(m, c):
                s, uses = res_use(m, c)
                if not (isinstance(m, int) and m == 0 and c < RES):
                    sp.wait_ge(res_out[s], (uses - 1) * 16)
                mt, half = c // 2, c % 2
                sp.dma_start(res[:, s, :], x[m, mt * P128:(mt + 1) * P128, half * HALF:(half + 1) * HALF]
                             ).then_inc(res_in[s], 16)

            def store_res(m, c):
                s, _ = res_use(m, c)
                mt, half = c // 2, c % 2
                sp.wait_ge(res_done, m * PROJ + c + 1)
                sp.dma_start(out[m, mt * P128:(mt + 1) * P128, half * HALF:(half + 1) * HALF], res[:, s, :]
                             ).then_inc(res_out[s], 16)

            for b in range(4):
                load_w_raw(b)
            load_x(0, 0)
            load_x(0, 1)
            for b in range(3 * PAIRS + KT):
                store_w(b)
                if b + 4 < 3 * PAIRS + KT:
                    load_w_raw(b + 4)
                if b < 4:
                    load_x(0, b + 2)
            load_x(0, 6)
            load_x(0, 7)
            for s in range(WRING):
                sp.wait_ge(w_stored[s], 16 * (3 * PAIRS + KT) // WRING)
            for b in range(3):
                load_w(b, b)
            copy_k(0, 0, 0)
            copy_k(0, 0, 1)

            def body(n, has_prev, has_next):
                blocks = block_list(has_prev, has_next)
                before = [("qkv", 0, 0), ("qkv", 0, 1), ("qkv", 0, 2)]
                if not (isinstance(n, int) and n == 0):
                    before = [("qkv", -1, 2)] + before
                issued = [0]

                def load_blocks(upto):
                    while issued[0] < min(upto, len(blocks)):
                        local = issued[0]
                        slot, _ = block_use(n, local)
                        prior = (before + blocks)[local + len(before) - WRING] if local + len(before) >= WRING else None
                        if prior is not None:
                            block_freed(sp, n, prior)
                        load_w(w_block(blocks[local]), slot)
                        issued[0] += 1

                for p in range(PAIRS):
                    P = n * PAIRS + p
                    used = 0
                    for i in range(TILES):
                        if p == 0 and i == 0:
                            load_blocks(4 if has_prev else 4)
                        if i == 2 and (p > 0 or has_prev):
                            spread_r(P - 1, (p - 1) % 2)
                        c = qkv_chunk_at(p, i - 1, has_next)
                        if c is not None and c % 2 == 1:
                            load_blocks(issued[0] + 1)
                        c = qkv_chunk_at(p, i - 2, has_next)
                        if c in (2, 3):
                            copy_k(P + 1, (p + 1) % 2, c - 2)
                        c = proj_chunk_at(p, i + 2, has_prev)
                        if c is not None:
                            load_res(n - 1, c)
                        c = proj_chunk_at(p, i - 1, has_prev)
                        if c is not None and c % 2 == 1:
                            load_blocks(issued[0] + 1)
                        c = proj_chunk_at(p, i - 1, has_prev)
                        if c is not None:
                            store_res(n - 1, c)
                        if p == 1 and i == 0 and has_prev:
                            store_res(n - 1, PROJ - 1)
                            load_blocks(issued[0] + 1)
                        if has_next and p == 1 and i + 1 in STAT_SLOTS:
                            load_x(n + 1, STAT_SLOTS.index(i + 1))
                        if has_next and p == 0 and i == TILES - 1:
                            load_x(n + 1, 0)
                        if has_next and p == 2 and i == 0:
                            load_x(n + 1, 4)
                            load_x(n + 1, 5)
                        if has_next and p == 2 and i - 3 in NORM_SLOTS[0:2]:
                            load_x(n + 1, 6 + NORM_SLOTS.index(i - 3))
                load_blocks(len(blocks))

            over_images(sp, body)
            for m in range(KT):
                u = 16 * N_IMG - 4 + m
                if m == 0:
                    block_freed(sp, LAST, ("proj", KT - 1))
                else:
                    block_freed(sp, LAST, ("qkv", 3, m - 1))
                load_w(3 * PAIRS + m, u % WRING)
            spread_r(PAIRS * N_IMG - 1, 1)
            for c in range(PROJ):
                load_res(LAST, c)
                if c >= 1:
                    store_res(LAST, c - 1)
            store_res(LAST, PROJ - 1)
            for s in range(RES):
                sp.wait_ge(res_out[s], 16 * N_IMG * PROJ // RES)

        @block.tensor
        def _(pe):
            fill_free = [None]

            def take_fill_bank(freed_by):
                if fill_free[0] is not None:
                    pe.wait_ge(*fill_free[0])
                fill_free[0] = freed_by

            def three_passes(w, hi, lo, cols):
                steps = [(k, wh, mov) for k in range(KT) for wh, mov in ((0, hi), (0, lo), (1, hi))]
                for j, (k, wh, mov) in enumerate(steps):
                    last = nc.tensor.matmul(ps_f[:], w_ring[:, w, wh, k, :], mov[:, k, cols],
                                            start=(j == 0), stop=(j == len(steps) - 1))
                return last

            def qkv_chunk(P, c, ring, loads):
                if c % 2 == 0:
                    pe.wait_ge(w_in[ring], loads * 16)
                half = c % 2
                take_fill_bank((qk_lo_done, P * 4 + c + 1) if c < 4 else (qkv_hi_done, P * CHUNKS + c + 1))
                three_passes(ring, h_hi, h_lo, slice(half * HALF, (half + 1) * HALF)).then_inc(qkv_done, 1)

            def h_ready(m):
                pe.wait_ge(h_hi_done, (m + 1) * KT)
                pe.wait_ge(h_lo_done, (m + 1) * KT)

            def proj_chunk(m, c, ring, loads):
                if c == 0:
                    pe.wait_ge(a_hi_done, (m + 1) * PAIRS)
                    pe.wait_ge(a_lo_done, (m + 1) * PAIRS)
                if c % 2 == 0:
                    pe.wait_ge(w_in[ring], loads * 16)
                half = c % 2
                take_fill_bank((res_done, m * PROJ + c + 1))
                three_passes(ring, a_hi, a_lo, slice(half * HALF, (half + 1) * HALF)).then_inc(proj_done, 1)

            def group_average(m, step):
                pe.wait_ge(gn_done, 3 * m + 1 + step)
                take_fill_bank((gn_done, 3 * m + 2 + step))
                nc.tensor.matmul(ps_f[:, 0:KT], avg[:], gsum[:], start=True, stop=True).then_inc(gavg_done, 1)

            def transpose_v(P, tiles_before):
                pe.wait_ge(qkv_hi_done, (P + 1) * CHUNKS)
                if tiles_before is not None:
                    pe.wait_ge(pt_lo_done, tiles_before)
                for t in range(ST):
                    last = nc.tensor.transpose(ps_t[:, t * P128:(t + 1) * P128], v32[:, t * P128:(t + 1) * P128], ident[:])
                last.then_inc(vtrans_done, 1)

            def transpose_p(P, i, v_before):
                pe.wait_ge(exp_done, P * TILES + i + 1)
                if v_before is not None:
                    pe.wait_ge(v_lo_done, v_before)
                elif i > 0 or not (isinstance(P, int) and P == 0):
                    pe.wait_ge(pt_lo_done, P * TILES + i)
                for t in range(ST):
                    last = nc.tensor.transpose(ps_t[:, t * P128:(t + 1) * P128], prob[:, i % 2, t * P128:(t + 1) * P128], ident[:])
                last.then_inc(ptrans_done, 1)

            def scores(P, par, i):
                if i == 0:
                    pe.wait_ge(qk_lo_done, (P + 1) * 4)
                    pe.wait_ge(k_copied, (P + 1) * 64)
                hd, t = i // ST, i % ST
                for half in range(2):
                    for hl in range(2):
                        last = nc.tensor.matmul(ps_s[:, i % 2, half * HALF:(half + 1) * HALF],
                                                Q[:, par, hd, t * P128:(t + 1) * P128],
                                                K[:, par, hd, hl, half * HALF:(half + 1) * HALF],
                                                start=(hl == 0), stop=(hl == 1))
                last.then_inc(scores_done, 1)

            def pv_group(P, par, g):
                pe.wait_ge(pt_lo_done, P * TILES + 2 * g + 2)
                if g == 0:
                    pe.wait_ge(v_lo_done, P + 1)
                if g > 0 or not (isinstance(P, int) and P == 0):
                    pe.wait_ge(o_add_done, P * GRP + g)
                for t in range(ST):
                    for j, pt in enumerate((pt_hi, pt_lo)):
                        last = nc.tensor.matmul(ps_o[:, 0:GW], V[:, par, t, g // 4, :], pt[:, g % 2, t, :],
                                                start=(t == 0 and j == 0), stop=(t == ST - 1 and j == 1))
                last.then_inc(pv_done, 1)

            def transpose_r(P):
                pe.wait_ge(rcp_done, P + 1)
                take_fill_bank((rcopy_done, P + 1))
                nc.tensor.transpose(ps_f[0:TILES, 0:P128], rcp[:], ident[:]).then_inc(rtrans_done, 1)

            pe.wait_ge(const_in, 96)
            group_average(0, 0)
            group_average(0, 1)
            h_ready(0)
            for c in range(CHUNKS):
                qkv_chunk(0, c, c // 2, 1)
            transpose_v(0, None)
            scores(0, 0, 0)
            scores(0, 0, 1)

            def body(n, has_prev, has_next):
                fill_free[0] = (qkv_hi_done, (n * PAIRS + 1) * CHUNKS)
                blocks = block_list(has_prev, has_next)
                for p in range(PAIRS):
                    P = n * PAIRS + p
                    for i in range(TILES):
                        first_tile = p == 0 and i == 0
                        v_before = None
                        if first_tile and isinstance(n, int) and n == 0:
                            v_before = 1
                        elif i == 0 and VT_SLOT[p - 1] == TILES - 1:
                            v_before = P + 1
                        elif i > 0 and vt_at(p, i - 1, has_next):
                            v_before = P + 2
                        transpose_p(P, i, v_before)
                        if i + 2 < TILES:
                            scores(P, p % 2, i + 2)
                        elif p < PAIRS - 1 or has_next:
                            scores(P + 1, (p + 1) % 2, i + 2 - TILES)
                        if i == 0 and (p > 0 or has_prev):
                            transpose_r(P - 1)
                            pv_group(P - 1, (p - 1) % 2, GRP - 1)
                        if i > 0 and i % 2 == 0:
                            pv_group(P, p % 2, i // 2 - 1)
                        c = qkv_chunk_at(p, i, has_next)
                        if c is not None:
                            if p == PAIRS - 1 and c == 0:
                                h_ready(n + 1)
                            ring, loads = block_use(n, blocks.index(("qkv", p + 1, c // 2)))
                            qkv_chunk(P + 1, c, ring, loads)
                        c = proj_chunk_at(p, i, has_prev)
                        if c is not None:
                            ring, loads = block_use(n, blocks.index(("proj", c // 2)))
                            proj_chunk(n - 1, c, ring, loads)
                        if p == 1 and has_next:
                            if i == GN_MEAN_SLOT:
                                group_average(n + 1, 0)
                            if i == GN_VAR_SLOT:
                                group_average(n + 1, 1)
                        if vt_at(p, i, has_next):
                            transpose_v(P + 1, P * TILES + i + 1)

            over_images(pe, body)
            last_pair = PAIRS * N_IMG - 1
            transpose_r(last_pair)
            pv_group(last_pair, (PAIRS - 1) % 2, GRP - 1)
            for c in range(PROJ):
                u = 16 * N_IMG - 4 + c // 2
                proj_chunk(LAST, c, u % WRING, u // WRING + 1)

        @block.scalar
        def _(act):
            def exp_tile(P, par, i):
                act.wait_ge(max_done, P * TILES + i + 1)
                if i == 0 and not (isinstance(P, int) and P < 2):
                    act.wait_ge(rcp_done, P - 1)
                nc.scalar.activation(prob[:, i % 2, :], ps_s[:, i % 2, :], ACT.Exp, bias=nmax[:, i % 2:i % 2 + 1],
                                     accum_out=rsum[:, par, i:i + 1]).then_inc(exp_done, 1)

            def pt_hi_tile(P, i):
                act.wait_ge(ptrans_done, P * TILES + i + 1)
                g = i // 2
                if i % 2 == 0 and (g >= 2 or not (isinstance(P, int) and P == 0)):
                    act.wait_ge(pv_done, P * GRP + g - 1)
                nc.scalar.copy(pt_hi[:, g % 2, :, (i % 2) * P128:(i % 2 + 1) * P128],
                               ps_t[:].rearrange("p (t s) -> p t s", s=P128)).then_inc(pt_hi_done, 1)

            def qkv_hi(P, par, p, c):
                t, half = c // 2, c % 2
                cols = slice(half * HALF, (half + 1) * HALF)
                act.wait_ge(qkv_done, P * CHUNKS + c + 1)
                b = 3 * p + t
                if t == 2:
                    nc.scalar.activation(v32[:, cols], ps_f[:], ACT.Identity, bias=b_qkv[:, b:b + 1]).then_inc(qkv_hi_done, 1)
                    return
                A = Q[0:D, par, 0, cols] if t == 0 else K[0:D, par, 0, 0, cols]
                B = Q[D:P128, par, 1, cols] if t == 0 else K[D:P128, par, 1, 0, cols]
                nc.scalar.activation(A, ps_f[0:D, :], ACT.Identity, bias=b_qkv[0:D, b:b + 1])
                nc.scalar.activation(B, ps_f[D:P128, :], ACT.Identity, bias=b_qkv[D:P128, b:b + 1]).then_inc(qkv_hi_done, 1)

            def v_hi(P, par):
                act.wait_ge(vtrans_done, P + 1)
                dst = V[:, par].rearrange("p t h c -> p (t h) c")[:, :, 0:D]
                nc.scalar.copy(dst, ps_t[:].rearrange("p (a c) -> p a c", c=D)).then_inc(v_hi_done, 1)

            def o_copy(P, g):
                act.wait_ge(pv_done, P * GRP + g + 1)
                if g // 4 == 0:
                    nc.scalar.copy(o_tmp[0:D, :], ps_o[D:P128, 0:GW]).then_inc(o_copy_done, 1)
                else:
                    nc.scalar.copy(o_tmp[D:P128, :], ps_o[0:D, 0:GW]).then_inc(o_copy_done, 1)

            def a_hi_pair(P, par, p):
                act.wait_ge(mul_done, P + 1)
                if p == 0 and not (isinstance(P, int) and P == 0):
                    act.wait_ge(proj_done, P * 2)
                nc.scalar.copy(a_hi[:, p, :], U[:, par, :]).then_inc(a_hi_done, 1)

            def h_hi_tile(m, k):
                act.wait_ge(h32_done, m * KT + k + 1)
                if k == 0 and not (isinstance(m, int) and m == 0):
                    act.wait_ge(qkv_done, m * PAIRS * CHUNKS)
                nc.scalar.copy(h_hi[:, k, :], x_t[:, k % 2, :]).then_inc(h_hi_done, 1)

            act.wait_ge(const_in, 96)
            for b in range(3 * PAIRS + KT):
                act.wait_ge(w_raw_in[b % 4], 16 * (b // 4 + 1))
                if b >= WRING:
                    act.wait_ge(w_stored[b % WRING], 16 * (b // WRING))
                src = prob[:, (b % 4) // 2, (b % 2) * HALF:(b % 2 + 1) * HALF]
                is_q = b < 3 * PAIRS and b % 3 == 0
                nc.scalar.mul(w_ring[:, b % WRING, 0].rearrange("p k o -> p (k o)"), src,
                              SCALE if is_q else 1.0).then_inc(w_hi_done, 1)
            for k in range(KT):
                h_hi_tile(0, k)
            act.wait_ge(bias_done, 1)
            for c in range(CHUNKS):
                qkv_hi(0, 0, 0, c)
            v_hi(0, 0)
            exp_tile(0, 0, 0)

            def body(n, has_prev, has_next):
                for p in range(PAIRS):
                    P = n * PAIRS + p
                    for i in range(TILES):
                        pt_hi_tile(P, i)
                        if i + 1 < TILES:
                            exp_tile(P, p % 2, i + 1)
                        elif p < PAIRS - 1 or has_next:
                            exp_tile(P + 1, (p + 1) % 2, 0)
                        if vt_at(p, i, has_next):
                            v_hi(P + 1, (p + 1) % 2)
                        if i == 1 and (p > 0 or has_prev):
                            o_copy(P - 1, GRP - 1)
                        if i >= 3 and i % 2 == 1:
                            o_copy(P, (i - 3) // 2)
                        c = qkv_chunk_at(p, i - 1, has_next)
                        if c is not None:
                            qkv_hi(P + 1, (p + 1) % 2, (p + 1) % PAIRS, c)
                        if i == 5 and (p > 0 or has_prev):
                            a_hi_pair(P - 1, (p - 1) % 2, (p - 1) % PAIRS)
                        if p == 2 and has_next and i in NORM_SLOTS:
                            h_hi_tile(n + 1, NORM_SLOTS.index(i))

            over_images(act, body)
            last_pair = PAIRS * N_IMG - 1
            o_copy(last_pair, GRP - 1)
            a_hi_pair(last_pair, 1, PAIRS - 1)

        @block.vector
        def _(dve):
            def as32(ap):
                return ap.bitcast(fp32)

            def max_tile(P, i):
                dve.wait_ge(scores_done, P * TILES + i + 1)
                nc.vector.tensor_reduce(nmax[:, i % 2:i % 2 + 1], ps_s[:, i % 2, :], AX, ALU.max,
                                        negate=True).then_inc(max_done, 1)

            def pt_lo_tile(P, i):
                dve.wait_ge(pt_hi_done, P * TILES + i + 1)
                g = i // 2
                cols = slice((i % 2) * P128, (i % 2 + 1) * P128)
                nc.vector.tensor_tensor(pt_lo[:, g % 2, :, cols], ps_t[:].rearrange("p (t s) -> p t s", s=P128),
                                        as32(pt_hi[:, g % 2, :, cols]), ALU.subtract).then_inc(pt_lo_done, 1)

            def qk_lo(P, par, p, c):
                t, half = c // 2, c % 2
                cols = slice(half * HALF, (half + 1) * HALF)
                b = 3 * p + t
                dve.wait_ge(qkv_hi_done, P * CHUNKS + c + 1)
                low, up = slice(0, D), slice(D, P128)
                for hd, own, other in ((0, low, up), (1, up, low)):
                    if t == 0:
                        dst, hi = Q[other, par, hd, cols], Q[own, par, hd, cols]
                    else:
                        dst, hi = K[own, par, hd, 1, cols], K[own, par, hd, 0, cols]
                    last = nc.vector.scalar_tensor_tensor(out=dst, in0=ps_f[own, :], scalar=b_qkv[own, b:b + 1],
                                                          in1=as32(hi), op0=ALU.add, op1=ALU.subtract)
                last.then_inc(qk_lo_done, 1)

            def v_lo(P, par):
                dve.wait_ge(v_hi_done, P + 1)
                both = V[:, par].rearrange("p t h c -> p (t h) c")
                nc.vector.tensor_tensor(both[:, :, D:2 * D], ps_t[:].rearrange("p (a c) -> p a c", c=D),
                                        as32(both[:, :, 0:D]), ALU.subtract).then_inc(v_lo_done, 1)

            def o_add(P, par, g):
                dve.wait_ge(o_copy_done, P * GRP + g + 1)
                if g == 0 and not (isinstance(P, int) and P < 2):
                    dve.wait_ge(a_lo_done, P - 1)
                own = slice(0, D) if g // 4 == 0 else slice(D, P128)
                nc.vector.tensor_tensor(U[own, par, (g % 4) * GW:(g % 4 + 1) * GW], ps_o[own, 0:GW], o_tmp[own, :],
                                        ALU.add).then_inc(o_add_done, 1)

            def recip(P, par):
                dve.wait_ge(exp_done, (P + 1) * TILES)
                if not (isinstance(P, int) and P == 0):
                    dve.wait_ge(rtrans_done, P)
                nc.vector.reciprocal(rcp[:], rsum[:, par, :]).then_inc(rcp_done, 1)

            def r_copy(P):
                dve.wait_ge(rtrans_done, P + 1)
                if not (isinstance(P, int) and P == 0):
                    dve.wait_ge(r_out, P * 16)
                nc.vector.tensor_copy(rT[:], ps_f[0:TILES, 0:P128]).then_inc(rcopy_done, 1)

            steps = [0]

            def link(ins, m, per=24):
                steps[0] += 1
                ins.then_inc(dve_step, 1)
                dve.wait_ge(dve_step, m * per + steps[0])

            GN_LINKS = 4 + 7

            def stats_tile(m, k):
                dve.wait_ge(x_in[k % 2], 16 * (m * KT + k // 2 + 1))
                for half in range(2):
                    ins = nc.vector.bn_stats(bn6[:, k, half, :], x_t[:, k % 2, half * HALF:(half + 1) * HALF])
                ins.then_inc(stat_done, 1)

            parts = bn6[:].rearrange("p k h (e f) -> p (k h e) f", f=3)
            means = parts[:, :, 1].rearrange("p (k e) -> p k e", e=4)

            def channel_means(m):
                dve.wait_ge(stat_done, (m + 1) * KT)
                nc.vector.tensor_reduce(gsum[:], means, AX, ALU.add).then_inc(gn_done, 1)

            def deviations(m):
                dve.wait_ge(gavg_done, 2 * m + 1)
                steps[0] = 0
                link(nc.vector.tensor_scalar(gmean[:], ps_f[:, 0:KT], 0.25, None, ALU.mult), m, GN_LINKS)
                every = gmean[:].rearrange("p (k o) -> p k o", o=1).broadcast_to((P128, KT, 4))
                link(nc.vector.tensor_tensor(gdev4[:], means, every, ALU.subtract), m, GN_LINKS)
                flat = gdev4[:].rearrange("p k e -> p (k e)")
                link(nc.vector.tensor_tensor(flat, flat, flat, ALU.mult), m, GN_LINKS)
                link(nc.vector.scalar_tensor_tensor(out=flat, in0=parts[:, :, 2], scalar=4.0 / S, in1=flat,
                                                    op0=ALU.mult, op1=ALU.add), m, GN_LINKS)
                nc.vector.tensor_reduce(gsum[:], gdev4[:], AX, ALU.add).then_inc(gn_done, 1)

            def group_variance(m):
                dve.wait_ge(gavg_done, 2 * m + 2)
                nc.vector.tensor_scalar(gvar[:], ps_f[:, 0:KT], 0.25, EPS, ALU.mult, ALU.add).then_inc(gn_done, 1)

            def coefficients(m):
                dve.wait_ge(root_done, m + 1)
                link(nc.vector.tensor_tensor(gvar[:], gvar[:], grs[:], ALU.mult), m, GN_LINKS)
                link(nc.vector.tensor_tensor(gvar[:], gvar[:], grs[:], ALU.mult), m, GN_LINKS)
                link(nc.vector.tensor_scalar(gvar[:], gvar[:], -0.5, 1.5, ALU.mult, ALU.add), m, GN_LINKS)
                link(nc.vector.tensor_tensor(gvar[:], grs[:], gvar[:], ALU.mult), m, GN_LINKS)
                link(nc.vector.tensor_tensor(gn_a[:], gvar[:], gn_w[:], ALU.mult), m, GN_LINKS)
                link(nc.vector.tensor_tensor(gdev[:], gmean[:], gn_a[:], ALU.mult), m, GN_LINKS)
                link(nc.vector.tensor_tensor(gn_c[:], gn_b[:], gdev[:], ALU.subtract), m, GN_LINKS)

            def h32_tile(m, k):
                dve.wait_ge(x_in[k % 2], 16 * (m * KT + 2 + k // 2 + 1))
                nc.vector.tensor_scalar(x_t[:, k % 2, :], x_t[:, k % 2, :], gn_a[:, k:k + 1], gn_c[:, k:k + 1],
                                        ALU.mult, ALU.add).then_inc(h32_done, 1)

            def proj_out(m, c):
                dve.wait_ge(proj_done, m * PROJ + c + 1)
                dve.wait_ge(res_in[c % RES], 16 * (m * (PROJ // RES) + c // RES + 1))
                nc.vector.scalar_tensor_tensor(out=res[:, c % RES, :], in0=ps_f[:], scalar=b_p[:, c // 2:c // 2 + 1],
                                               in1=res[:, c % RES, :], op0=ALU.add, op1=ALU.add).then_inc(res_done, 1)

            dve.wait_ge(const_in, 96)
            for p in range(PAIRS):
                last = nc.vector.tensor_scalar(b_qkv[:, 3 * p:3 * p + 1], b_qkv[:, 3 * p:3 * p + 1], SCALE, None, ALU.mult)
            last.then_inc(bias_done, 1)

            def w_lo(b):
                dve.wait_ge(w_hi_done, b + 1)
                src = prob[:, (b % 4) // 2, (b % 2) * HALF:(b % 2 + 1) * HALF]
                hi = w_ring[:, b % WRING, 0].rearrange("p k o -> p (k o)")
                lo = w_ring[:, b % WRING, 1].rearrange("p k o -> p (k o)")
                is_q = b < 3 * PAIRS and b % 3 == 0
                nc.vector.scalar_tensor_tensor(out=lo, in0=src, scalar=SCALE if is_q else 1.0, in1=as32(hi),
                                               op0=ALU.mult, op1=ALU.subtract).then_inc(w_lo_done, 1)

            for b in range(3 * PAIRS + KT):
                w_lo(b)
                if b % 2 == 1 and b // 2 < KT:
                    stats_tile(0, b // 2)
                if b == 10:
                    channel_means(0)
                    deviations(0)
                    group_variance(0)
                    coefficients(0)
            for k in range(KT):
                h32_tile(0, k)
            dve.wait_ge(bias_done, 1)
            for c in range(4):
                qk_lo(0, 0, 0, c)
            v_lo(0, 0)
            max_tile(0, 0)

            def body(n, has_prev, has_next):
                for p in range(PAIRS):
                    P = n * PAIRS + p
                    for i in range(TILES):
                        if i == 0 and (p > 0 or has_prev):
                            recip(P - 1, (p - 1) % 2)
                        if i + 1 < TILES:
                            max_tile(P, i + 1)
                        elif p < PAIRS - 1 or has_next:
                            max_tile(P + 1, 0)
                        pt_lo_tile(P, i)
                        if vt_at(p, i, has_next):
                            v_lo(P + 1, (p + 1) % 2)
                        if p == 1 and i == 0 and has_prev:
                            proj_out(n - 1, PROJ - 1)
                        if i == 0 and (p > 0 or has_prev):
                            r_copy(P - 1)
                        if i == 1 and (p > 0 or has_prev):
                            o_add(P - 1, (p - 1) % 2, GRP - 1)
                        if i >= 3 and i % 2 == 1:
                            o_add(P, p % 2, (i - 3) // 2)
                        c = qkv_chunk_at(p, i - 1, has_next)
                        if c is not None and c < 4:
                            qk_lo(P + 1, (p + 1) % 2, (p + 1) % PAIRS, c)
                        c = proj_chunk_at(p, i - 1, has_prev)
                        if c is not None:
                            proj_out(n - 1, c)
                        if p == 1 and has_next:
                            if i in STAT_SLOTS:
                                stats_tile(n + 1, STAT_SLOTS.index(i))
                            if i == STAT_SLOTS[-1]:
                                channel_means(n + 1)
                            if i == GN_MEAN_SLOT + 1:
                                deviations(n + 1)
                            if i == GN_VAR_SLOT + 1:
                                group_variance(n + 1)
                            if i == GN_VAR_SLOT + 2:
                                coefficients(n + 1)
                        if p == 2 and has_next and i + 1 in NORM_SLOTS:
                            h32_tile(n + 1, NORM_SLOTS.index(i + 1))

            over_images(dve, body)
            last_pair = PAIRS * N_IMG - 1
            recip(last_pair, 1)
            r_copy(last_pair)
            o_add(last_pair, 1, GRP - 1)
            for c in range(PROJ):
                proj_out(LAST, c)

        @block.gpsimd
        def _(pool):
            def h_lo_tile(m, k):
                pool.wait_ge(h_hi_done, m * KT + k + 1)
                nc.gpsimd.tensor_tensor(h_lo[:, k, :], x_t[:, k % 2, :], h_hi[:, k, :].bitcast(fp32),
                                        ALU.subtract).then_inc(h_lo_done, 1)

            def normalise_pair(P, par, p):
                pool.wait_ge(r_in, (P + 1) * 32)
                pool.wait_ge(o_add_done, (P + 1) * GRP)
                nc.gpsimd.tensor_tensor(U[:, par, :], U[:, par, :], R[:], ALU.mult).then_inc(mul_done, 1)
                pool.wait_ge(a_hi_done, P + 1)
                nc.gpsimd.tensor_tensor(a_lo[:, p, :], U[:, par, :], a_hi[:, p, :].bitcast(fp32),
                                        ALU.subtract).then_inc(a_lo_done, 1)

            def root(m):
                pool.wait_ge(gn_done, 3 * m + 3)
                nc.gpsimd.tensor_tensor(grs[:], gvar[:], m_half[:], ALU.pow).then_inc(root_done, 1)

            nc.gpsimd.memset(m_half[:], -0.5).then_inc(half_set, 1)
            pool.wait_ge(half_set, 1)
            root(0)
            for k in range(KT):
                h_lo_tile(0, k)

            def body(n, has_prev, has_next):
                for p in range(PAIRS):
                    P = n * PAIRS + p
                    if p > 0 or has_prev:
                        normalise_pair(P - 1, (p - 1) % 2, (p - 1) % PAIRS)
                    if p == 1 and has_next:
                        root(n + 1)
                    if p == 2 and has_next:
                        for k in range(KT):
                            h_lo_tile(n + 1, k)

            over_images(pool, body)
            normalise_pair(PAIRS * N_IMG - 1, 1, PAIRS - 1)


def kernel(x, L0_conv_norm_w, L0_conv_norm_b, L0_conv_qkv_w, L0_conv_qkv_b, L0_conv_proj_w, L0_conv_proj_b):
    import numpy as np
    import concourse.bacc as bacc
    from concourse.bass_utils import run_bass_kernel_spmd

    x, nw, nb, qw, qb, pw, pb = (np.asarray(a) for a in (
        x, L0_conv_norm_w, L0_conv_norm_b, L0_conv_qkv_w, L0_conv_qkv_b, L0_conv_proj_w, L0_conv_proj_b))
    group = C // 32
    arrays = {
        "x": np.ascontiguousarray(x.reshape(N_IMG, C, S)),
        "wqkvT": np.ascontiguousarray(qw.T),
        "bqkv": np.ascontiguousarray(qb.reshape(3, PAIRS, P128).transpose(2, 1, 0).reshape(P128, 3 * PAIRS)),
        "wpT": np.ascontiguousarray(pw.T),
        "bp": np.ascontiguousarray(pb.reshape(KT, P128).T),
        "gnw": np.ascontiguousarray(nw.reshape(KT, P128).T),
        "gnb": np.ascontiguousarray(nb.reshape(KT, P128).T),
        "ident_in": np.eye(P128, dtype=np.float32),
        "avg_in": np.kron(np.eye(P128 // group, dtype=np.float32), np.full((group, group), 1.0 / group, np.float32)),
    }
    nc = bacc.Bacc("TRN2", target_bir_lowering=False, num_devices=1, dynamic_dma_scratch_size=1024)
    aps = [nc.dram_tensor(n, a.shape, mybir.dt.from_np(a.dtype), kind="ExternalInput").ap() for n, a in arrays.items()]
    out = nc.dram_tensor("out", (N_IMG, C, S), mybir.dt.float32, kind="ExternalOutput").ap()
    build(nc, *aps, out)
    r = run_bass_kernel_spmd(nc, [arrays], core_ids=[0])
    return r.results[0]["out"].reshape(N_IMG, C, 32, 32)
```

```python
from contextlib import ExitStack

import concourse.bass as bass
from concourse import mybir

N_IMG, C, S = 16, 512, 1024
HEADS, D = 8, 64
P128 = 128
KT = C // P128
PAIRS = HEADS // 2
ST = S // P128
TILES = 2 * ST
GRP = 8
GW = 256
HALF = 512
EPS = 1e-5
SCALE = D ** -0.5
CHUNKS = 6
COLUMN = (1, 2, 0)
PIECES = 4
PROJ = 2 * KT
RES = 2
WRING = 2
WSTAGE = 8
LAST = N_IMG - 1

QKV_SLOTS = [16 * p + i for p in range(3) for i in (1, 3, 5, 7, 9, 11)] + [48 + i for i in (5, 6, 7, 8, 10, 12)]
VT_SLOTS = [16 * p + i for p in range(4) for i in (8, 10, 12, 14)]
PROJ_SLOTS = [13, 15, 29, 31, 45, 47, 49, 51]
STAT_SLOTS = [7, 9, 11, 13]
GN_MEAN_SLOT, GN_VAR_SLOT = 18, 20
NORM_SLOTS = [44, 46, 49, 51]
A_HI_SLOTS = [8, 53, 55, 57]
X_SLOTS = [33, 34, 47, 50]


def found(slots, q):
    return slots.index(q) if q in slots else None


def qkv_at(q, has_next):
    j = found(QKV_SLOTS, q)
    return None if j is None or (j >= 18 and not has_next) else (j // CHUNKS + 1, j % CHUNKS)


def proj_at(q, has_prev):
    return found(PROJ_SLOTS, q) if has_prev else None


def vt_at(q, has_next):
    j = found(VT_SLOTS, q)
    return None if j is None or (j >= 12 and not has_next) else (j // PIECES + 1, j % PIECES)


def block_list(has_prev, has_next):
    out = []
    for q in range(PAIRS * TILES):
        if (j := qkv_at(q, has_next)) is not None and j[1] % 2 == 0:
            out.append(("qkv", j[0], j[1] // 2))
        if (c := proj_at(q, has_prev)) is not None and c % 2 == 0:
            out.append(("proj", c // 2))
    return out


def block_use(n, local):
    if isinstance(n, int) and n == 0:
        u = 3 + local
        return u % WRING, u // WRING + 1
    return (local - 1) % WRING, n * (16 // WRING) + ((local - 1) // WRING + 1)


def build(nc, x, wqkvT, bqkv, wpT, bp, gnw, gnb, ident_in, avg_in, out):
    fp32, f32r = mybir.dt.float32, mybir.dt.float32r
    ACT = mybir.ActivationFunctionType
    ALU = mybir.AluOpType
    AX = mybir.AxisListType.X

    w_scr = nc.dram_tensor("w_scr", [3 * PAIRS + KT, P128, 2 * KT * P128], fp32, kind="Internal").ap()
    r_scr = nc.dram_tensor("r_scr", [2, 2, S], fp32, kind="Internal").ap()

    with ExitStack() as ctx:
        def sb(name, shape, dt=fp32):
            return ctx.enter_context(nc.sbuf_tensor(name, shape, dt))

        def sem(name):
            return ctx.enter_context(nc.semaphore(name))

        h_hi = sb("h_hi", [P128, KT, S], f32r)
        h_lo = sb("h_lo", [P128, KT, S], f32r)
        w_ring = sb("w_ring", [P128, WRING, 2, KT, P128], f32r)
        Q = sb("Q", [P128, 2, 2, S], f32r)
        K = sb("K", [P128, 2, 2, 2, S], f32r)
        V = sb("V", [P128, 2, ST, 2, 2 * D], f32r)
        pt_hi = sb("pt_hi", [P128, 2, ST, GW], f32r)
        pt_lo = sb("pt_lo", [P128, 2, ST, GW], f32r)
        prob = sb("prob", [P128, 2, S])
        a_hi = sb("a_hi", [P128, KT, S], f32r)
        a_lo = sb("a_lo", [P128, KT, S], f32r)
        x_t = sb("x_t", [P128, 2, S])
        U = sb("U", [P128, PAIRS, S])
        R = sb("R", [P128, S])
        v32 = sb("v32", [P128, S])
        kq32 = sb("kq32", [P128, 2, HALF])
        o_tmp = sb("o_tmp", [P128, GW])
        res = sb("res", [P128, RES, HALF])
        ident = sb("ident", [P128, P128])
        avg = sb("avg", [P128, P128])
        b_qkv = sb("b_qkv", [P128, 3 * PAIRS])
        b_p = sb("b_p", [P128, KT])
        gn_w = sb("gn_w", [P128, KT])
        gn_b = sb("gn_b", [P128, KT])
        nmax = sb("nmax", [P128, 2])
        rsum = sb("rsum", [P128, 2, TILES])
        rcp = sb("rcp", [P128, TILES])
        rT = sb("rT", [TILES, P128])
        bn6 = sb("bn6", [P128, KT, 2, 6])
        gsum = sb("gsum", [P128, KT])
        gdev4 = sb("gdev4", [P128, KT, 4])
        gmean = sb("gmean", [P128, KT])
        gdev = sb("gdev", [P128, KT])
        gvar = sb("gvar", [P128, KT])
        grs = sb("grs", [P128, KT])
        m_half = sb("m_half", [P128, KT])
        one = sb("one", [P128, 1])
        gn_a = sb("gn_a", [P128, KT])
        gn_c = sb("gn_c", [P128, KT])

        ps_s = ctx.enter_context(nc.psum_tensor("ps_s", [P128, 2, S], fp32))
        ps_t = ctx.enter_context(nc.psum_tensor("ps_t", [P128, S], fp32))
        ps_o = ctx.enter_context(nc.psum_tensor("ps_o", [P128, HALF], fp32))
        ps_f = ctx.enter_context(nc.psum_tensor("ps_f", [P128, HALF], fp32))

        scores_done = sem("scores_done")
        ptrans_done = sem("ptrans_done")
        pv_done = sem("pv_done")
        qkv_done = sem("qkv_done")
        vtrans_done = sem("vtrans_done")
        proj_done = sem("proj_done")
        rtrans_done = sem("rtrans_done")
        gavg_done = sem("gavg_done")
        exp_done = sem("exp_done")
        pt_hi_done = sem("pt_hi_done")
        qkv32_done = sem("qkv32_done")
        v_hi_done = sem("v_hi_done")
        o_copy_done = sem("o_copy_done")
        a_hi_done = sem("a_hi_done")
        h_hi_done = sem("h_hi_done")
        w_hi_done = sem("w_hi_done")
        max_done = sem("max_done")
        pt_lo_done = sem("pt_lo_done")
        v_lo_done = sem("v_lo_done")
        o_add_done = sem("o_add_done")
        rcp_done = sem("rcp_done")
        rcopy_done = sem("rcopy_done")
        stat_done = sem("stat_done")
        gn_read = sem("gn_read")
        gn_done = sem("gn_done")
        h32_done = sem("h32_done")
        res_done = sem("res_done")
        w_lo_done = sem("w_lo_done")
        bias_done = sem("bias_done")
        dve_step = sem("dve_step")
        root_done = sem("root_done")
        kq_hi_done = sem("kq_hi_done")
        split_done = sem("split_done")
        mul_done = sem("mul_done")
        a_lo_done = sem("a_lo_done")
        h_lo_done = sem("h_lo_done")
        half_set = sem("half_set")
        const_in = sem("const_in")
        w_raw_in = [sem(f"w_raw_in{i}") for i in range(4)]
        w_stored = [sem(f"w_stored{i}") for i in range(WSTAGE)]
        w_in = [sem(f"w_in{i}") for i in range(WRING)]
        k_copied = sem("k_copied")
        q_moved = [sem(f"q_moved{i}") for i in range(2)]
        x_in = [sem(f"x_in{i}") for i in range(2)]
        r_out = sem("r_out")
        r_in = sem("r_in")
        res_in = [sem(f"res_in{i}") for i in range(RES)]
        res_out = [sem(f"res_out{i}") for i in range(RES)]

        block = ctx.enter_context(nc.Block())

        def over_images(eng, body):
            body(0, False, True)
            with eng.Fori(1, LAST) as n:
                body(n, True, True)
            body(LAST, True, False)

        def w_stage(b):
            return (a_hi, a_lo)[b // 4 % 2][:, b % 4, :]

        def w_block(kind):
            return 3 * (kind[1] % PAIRS) + COLUMN[kind[2]] if kind[0] == "qkv" else 3 * PAIRS + kind[1]

        def block_freed(eng, n, kind):
            if kind[0] == "qkv":
                eng.wait_ge(qkv_done, (n * PAIRS + kind[1]) * CHUNKS + 2 * (kind[2] + 1))
            else:
                eng.wait_ge(proj_done, (n - 1) * PROJ + 2 * (kind[1] + 1))

        @block.sync
        def _(sp):
            sp.dma_start(ident[:], ident_in).then_inc(const_in, 16)
            sp.dma_start(avg[:], avg_in).then_inc(const_in, 16)
            sp.dma_start(b_qkv[:], bqkv).then_inc(const_in, 16)
            sp.dma_start(b_p[:], bp).then_inc(const_in, 16)
            sp.dma_start(gn_w[:], gnw).then_inc(const_in, 16)
            sp.dma_start(gn_b[:], gnb).then_inc(const_in, 16)

            def load_x(m, use):
                k, s = use % KT, use % 2
                if use in (0, 1):
                    if not (isinstance(m, int) and m == 0):
                        sp.wait_ge(h_lo_done, KT * m - 1 + use)
                elif use < 6:
                    sp.wait_ge(stat_done, KT * m + use - 1)
                else:
                    sp.wait_ge(h_lo_done, KT * m + use - 5)
                sp.dma_start(x_t[:, s, :], x[m, k * P128:(k + 1) * P128, :]).then_inc(x_in[s], 16)

            def load_w_raw(b):
                p, t = b // 3, b % 3
                if b < 3 * PAIRS:
                    src = wqkvT[:, t * C + p * P128:t * C + (p + 1) * P128]
                else:
                    m = b - 3 * PAIRS
                    src = wpT[:, m * P128:(m + 1) * P128]
                if b >= 4:
                    sp.wait_ge(w_lo_done, b - 3)
                dst = prob[:, (b % 4) // 2, (b % 2) * HALF:(b % 2 + 1) * HALF]
                sp.dma_start(dst.rearrange("p (k o) -> p k o", k=KT),
                             src.rearrange("(k p) o -> p k o", p=P128)).then_inc(w_raw_in[b % 4], 16)

            def store_w(b):
                sp.wait_ge(w_hi_done, b + 1)
                sp.wait_ge(w_lo_done, b + 1)
                sp.dma_start(w_scr[b], w_stage(b).bitcast(fp32)).then_inc(w_stored[b % WSTAGE], 16)

            def load_w(b, slot):
                sp.dma_start(w_ring[:, slot].rearrange("p a k o -> p (a k o)").bitcast(fp32), w_scr[b]).then_inc(w_in[slot], 16)

            def copy_k(P, par, half):
                sp.wait_ge(split_done, P * 4 + 1 + half)
                cols = slice(half * HALF, (half + 1) * HALF)
                sp.dma_start(K[D:P128, par, 0, :, cols].bitcast(fp32), K[0:D, par, 0, :, cols].bitcast(fp32)).then_inc(k_copied, 16)
                sp.dma_start(K[0:D, par, 1, :, cols].bitcast(fp32), K[D:P128, par, 1, :, cols].bitcast(fp32)).then_inc(k_copied, 16)

            def move_q(P, par, half):
                sp.wait_ge(split_done, P * 4 + 3 + half)
                cols = slice(half * HALF, (half + 1) * HALF)
                sp.dma_start(Q[D:P128, par, 0, cols].bitcast(fp32), kq32[0:D, half, :]).then_inc(q_moved[half], 16)
                sp.dma_start(Q[0:D, par, 1, cols].bitcast(fp32), kq32[D:P128, half, :]).then_inc(q_moved[half], 16)

            def spread_r(P, par):
                sp.wait_ge(rcopy_done, P + 1)
                sp.dma_start(r_scr[par].rearrange("h (t s) -> (h t) s", s=P128), rT[:]).then_inc(r_out, 16)
                sp.wait_ge(r_out, (P + 1) * 16)
                sp.dma_start(R[0:D, :], r_scr[par, 0:1, :].broadcast_to((D, S))).then_inc(r_in, 16)
                sp.dma_start(R[D:P128, :], r_scr[par, 1:2, :].broadcast_to((D, S))).then_inc(r_in, 16)

            def res_use(m, c):
                return c % RES, m * (PROJ // RES) + c // RES + 1

            def load_res(m, c):
                s, uses = res_use(m, c)
                if not (isinstance(m, int) and m == 0 and c < RES):
                    sp.wait_ge(res_out[s], (uses - 1) * 16)
                mt, half = c // 2, c % 2
                sp.dma_start(res[:, s, :], x[m, mt * P128:(mt + 1) * P128, half * HALF:(half + 1) * HALF]
                             ).then_inc(res_in[s], 16)

            def store_res(m, c):
                s, _ = res_use(m, c)
                mt, half = c // 2, c % 2
                sp.wait_ge(res_done, m * PROJ + c + 1)
                sp.dma_start(out[m, mt * P128:(mt + 1) * P128, half * HALF:(half + 1) * HALF], res[:, s, :]
                             ).then_inc(res_out[s], 16)

            for b in range(4):
                load_w_raw(b)
            load_x(0, 0)
            load_x(0, 1)
            for b in range(3 * PAIRS + KT):
                store_w(b)
                if b + 4 < 3 * PAIRS + KT:
                    load_w_raw(b + 4)
                if b < 4:
                    load_x(0, b + 2)
            load_x(0, 6)
            load_x(0, 7)
            for s in range(WSTAGE):
                sp.wait_ge(w_stored[s], 16 * (3 * PAIRS + KT) // WSTAGE)
            for b in range(3):
                if b >= WRING:
                    block_freed(sp, 0, ("qkv", 0, b - WRING))
                load_w(COLUMN[b], b % WRING)
            for half in range(2):
                copy_k(0, 0, half)
            for half in range(2):
                move_q(0, 0, half)
            for t in range(WRING):
                block_freed(sp, 0, ("qkv", 0, 3 - WRING + t))
                load_w(w_block(("qkv", 1, t)), (3 + t) % WRING)

            def body(n, has_prev, has_next):
                blocks = block_list(has_prev, has_next)
                following = ([("qkv", 1, 0), ("qkv", 1, 1)] if has_next else [("proj", 0), ("proj", 1)])
                blocks_from = blocks + following

                def load_after(local):
                    block_freed(sp, n, blocks[local])
                    nxt = local + WRING
                    if nxt < len(blocks):
                        slot = block_use(n, nxt)[0]
                    elif has_next:
                        slot = block_use(n + 1, nxt - len(blocks))[0]
                    else:
                        slot = (16 * N_IMG - 4 + nxt - len(blocks)) % WRING
                    load_w(w_block(blocks_from[nxt]), slot)

                for q in range(PAIRS * TILES):
                    p, i = q // TILES, q % TILES
                    P = n * PAIRS + p
                    if i == 2 and (p > 0 or has_prev):
                        spread_r(P - 1, (p - 1) % 2)
                    if (j := qkv_at(q - 1, has_next)) is not None and j[1] % 2 == 1:
                        load_after(blocks.index(("qkv", j[0], j[1] // 2)))
                    if (c := proj_at(q - 1, has_prev)) is not None and c % 2 == 1:
                        load_after(blocks.index(("proj", c // 2)))
                    if (j := qkv_at(q - 2, has_next)) is not None:
                        if j[1] < 2:
                            copy_k(n * PAIRS + j[0], j[0] % 2, j[1])
                        elif j[1] >= 4:
                            move_q(n * PAIRS + j[0], j[0] % 2, j[1] - 4)
                    if (c := proj_at(q - 2, has_prev)) is not None:
                        store_res(n - 1, c)
                    if (c := proj_at(q + 1, has_prev)) is not None:
                        load_res(n - 1, c)
                    if has_next:
                        if (k := found(STAT_SLOTS, q + 1)) is not None:
                            load_x(n + 1, k)
                        if (k := found(X_SLOTS, q)) is not None:
                            load_x(n + 1, KT + k)

            over_images(sp, body)
            spread_r(PAIRS * N_IMG - 1, 1)
            for c in range(RES):
                load_res(LAST, c)
            for c in range(PROJ):
                m = c // 2 + WRING
                if c % 2 == 1 and m < KT:
                    block_freed(sp, LAST + 1, ("proj", c // 2))
                    load_w(3 * PAIRS + m, (16 * N_IMG - 4 + m) % WRING)
                store_res(LAST, c)
                if c + RES < PROJ:
                    load_res(LAST, c + RES)
            for s in range(RES):
                sp.wait_ge(res_out[s], 16 * N_IMG * PROJ // RES)

        @block.tensor
        def _(pe):
            o_free = [None]
            fill_free = [None]

            def take_fill_bank(freed_by):
                if fill_free[0] is not None:
                    pe.wait_ge(*fill_free[0])
                fill_free[0] = freed_by

            def three_passes(w, hi, lo, cols):
                steps = [(k, wh, mov) for k in range(KT) for wh, mov in ((0, hi), (0, lo), (1, hi))]
                for j, (k, wh, mov) in enumerate(steps):
                    last = nc.tensor.matmul(ps_f[:], w_ring[:, w, wh, k, :], mov[:, k, cols],
                                            start=(j == 0), stop=(j == len(steps) - 1))
                return last

            def qkv_chunk(P, c, ring, loads):
                if c % 2 == 0:
                    pe.wait_ge(w_in[ring], loads * 16)
                half = c % 2
                take_fill_bank((qkv32_done, P * CHUNKS + c + 1))
                three_passes(ring, h_hi, h_lo, slice(half * HALF, (half + 1) * HALF)).then_inc(qkv_done, 1)

            def h_ready(m):
                pe.wait_ge(h_hi_done, (m + 1) * KT)
                pe.wait_ge(h_lo_done, (m + 1) * KT)

            def proj_chunk(m, c, ring, loads):
                if c == 0:
                    pe.wait_ge(a_hi_done, (m + 1) * PAIRS)
                    pe.wait_ge(a_lo_done, (m + 1) * PAIRS)
                if c % 2 == 0:
                    pe.wait_ge(w_in[ring], loads * 16)
                half = c % 2
                take_fill_bank((res_done, m * PROJ + c + 1))
                three_passes(ring, a_hi, a_lo, slice(half * HALF, (half + 1) * HALF)).then_inc(proj_done, 1)

            def group_average(m, step):
                pe.wait_ge(gn_done, 2 * m + 1 + step)
                o_free[0] = (gn_read, 2 * m + 1 + step)
                nc.tensor.matmul(ps_o[:, GW:GW + KT], avg[:], gsum[:], start=True, stop=True).then_inc(gavg_done, 1)

            def transpose_v(P, piece):
                pe.wait_ge(qkv32_done, P * CHUNKS + 3 + piece // 2)
                o_free[0] = (v_lo_done, P * PIECES + piece + 1)
                for j in range(2):
                    t = 2 * piece + j
                    last = nc.tensor.transpose(ps_o[:, GW + j * P128:GW + (j + 1) * P128], v32[:, t * P128:(t + 1) * P128], ident[:])
                last.then_inc(vtrans_done, 1)

            def transpose_p(P, i):
                if i > 0 or not (isinstance(P, int) and P == 0):
                    pe.wait_ge(pt_lo_done, P * TILES + i)
                for t in range(ST):
                    last = nc.tensor.transpose(ps_t[:, t * P128:(t + 1) * P128], prob[:, i % 2, t * P128:(t + 1) * P128], ident[:])
                last.then_inc(ptrans_done, 1)

            def scores(P, par, i):
                if i == 0:
                    pe.wait_ge(k_copied, (P + 1) * 64)
                    pe.wait_ge(q_moved[0], (P + 1) * 32)
                if i == ST // 2:
                    pe.wait_ge(q_moved[1], (P + 1) * 32)
                hd, t = i // ST, i % ST
                for half in range(2):
                    for hl in range(2):
                        last = nc.tensor.matmul(ps_s[:, i % 2, half * HALF:(half + 1) * HALF],
                                                Q[:, par, hd, t * P128:(t + 1) * P128],
                                                K[:, par, hd, hl, half * HALF:(half + 1) * HALF],
                                                start=(hl == 0), stop=(hl == 1))
                last.then_inc(scores_done, 1)

            def pv_group(P, par, g):
                pe.wait_ge(pt_lo_done, P * TILES + 2 * g + 2)
                if g == 0:
                    pe.wait_ge(v_lo_done, (P + 1) * PIECES)
                if o_free[0] is not None:
                    pe.wait_ge(*o_free[0])
                    o_free[0] = None
                if g > 0 or not (isinstance(P, int) and P == 0):
                    pe.wait_ge(o_add_done, P * GRP + g)
                for t in range(ST):
                    for j, pt in enumerate((pt_hi, pt_lo)):
                        last = nc.tensor.matmul(ps_o[:, 0:GW], V[:, par, t, g // 4, :], pt[:, g % 2, t, :],
                                                start=(t == 0 and j == 0), stop=(t == ST - 1 and j == 1))
                last.then_inc(pv_done, 1)

            def transpose_r(P):
                pe.wait_ge(rcp_done, P + 1)
                o_free[0] = (rcopy_done, P + 1)
                nc.tensor.transpose(ps_o[0:TILES, GW:GW + P128], rcp[:], ident[:]).then_inc(rtrans_done, 1)

            pe.wait_ge(const_in, 96)
            group_average(0, 0)
            pe.wait_ge(gn_read, 1)
            group_average(0, 1)
            pe.wait_ge(gn_read, 2)
            h_ready(0)
            for c in range(CHUNKS):
                qkv_chunk(0, c, c // 2 % WRING, c // 2 // WRING + 1)
            for piece in range(PIECES):
                if piece > 0:
                    pe.wait_ge(v_lo_done, piece)
                transpose_v(0, piece)
            scores(0, 0, 0)
            scores(0, 0, 1)

            def body(n, has_prev, has_next):
                fill_free[0] = (qkv32_done, (n * PAIRS + 1) * CHUNKS)
                o_free[0] = (v_lo_done, (n * PAIRS + 1) * PIECES)
                blocks = block_list(has_prev, has_next)
                for q in range(PAIRS * TILES):
                    p, i = q // TILES, q % TILES
                    P = n * PAIRS + p
                    pe.wait_ge(exp_done, P * TILES + i + 1)
                    if i + 2 < TILES:
                        scores(P, p % 2, i + 2)
                    elif p < PAIRS - 1 or has_next:
                        scores(P + 1, (p + 1) % 2, i + 2 - TILES)
                    transpose_p(P, i)
                    if i == 0 and (p > 0 or has_prev):
                        pv_group(P - 1, (p - 1) % 2, GRP - 1)
                        transpose_r(P - 1)
                    if i > 0 and i % 2 == 0:
                        pv_group(P, p % 2, i // 2 - 1)
                    if has_next and q in (GN_MEAN_SLOT, GN_VAR_SLOT):
                        group_average(n + 1, (GN_MEAN_SLOT, GN_VAR_SLOT).index(q))
                    if (j := vt_at(q, has_next)) is not None:
                        transpose_v(n * PAIRS + j[0], j[1])
                    if (j := qkv_at(q, has_next)) is not None:
                        if j == (PAIRS, 0):
                            h_ready(n + 1)
                        qkv_chunk(n * PAIRS + j[0], j[1], *block_use(n, blocks.index(("qkv", j[0], j[1] // 2))))
                    if (c := proj_at(q, has_prev)) is not None:
                        proj_chunk(n - 1, c, *block_use(n, blocks.index(("proj", c // 2))))

            over_images(pe, body)
            last_pair = PAIRS * N_IMG - 1
            pv_group(last_pair, (PAIRS - 1) % 2, GRP - 1)
            transpose_r(last_pair)
            for c in range(PROJ):
                u = 16 * N_IMG - 4 + c // 2
                proj_chunk(LAST, c, u % WRING, u // WRING + 1)

        @block.scalar
        def _(act):
            def exp_tile(P, par, i):
                act.wait_ge(max_done, P * TILES + i + 1)
                if i == 0 and not (isinstance(P, int) and P < 2):
                    act.wait_ge(rcp_done, P - 1)
                nc.scalar.activation(prob[:, i % 2, :], ps_s[:, i % 2, :], ACT.Exp, bias=nmax[:, i % 2:i % 2 + 1],
                                     accum_out=rsum[:, par, i:i + 1]).then_inc(exp_done, 1)

            def pt_hi_tile(P, i):
                act.wait_ge(ptrans_done, P * TILES + i + 1)
                g = i // 2
                if i % 2 == 0 and (g >= 2 or not (isinstance(P, int) and P == 0)):
                    act.wait_ge(pv_done, P * GRP + g - 1)
                nc.scalar.copy(pt_hi[:, g % 2, :, (i % 2) * P128:(i % 2 + 1) * P128],
                               ps_t[:].rearrange("p (t s) -> p t s", s=P128)).then_inc(pt_hi_done, 1)

            def qkv32(P, p, c):
                t, half = c // 2, c % 2
                cols = slice(half * HALF, (half + 1) * HALF)
                b = 3 * p + COLUMN[t]
                act.wait_ge(qkv_done, P * CHUNKS + c + 1)
                if t == 0 and not (isinstance(P, int) and P == 0):
                    act.wait_ge(q_moved[half], P * 32)
                if t == 2:
                    act.wait_ge(split_done, P * 4 + 1 + half)
                nc.scalar.activation(v32[:, cols] if t == 1 else kq32[:, half, :], ps_f[:], ACT.Identity,
                                     bias=b_qkv[:, b:b + 1]).then_inc(qkv32_done, 1)

            def v_hi(P, par, piece):
                act.wait_ge(vtrans_done, P * PIECES + piece + 1)
                dst = V[:, par, 2 * piece:2 * piece + 2].rearrange("p t h c -> p (t h) c")[:, :, 0:D]
                nc.scalar.copy(dst, ps_o[:, GW:2 * GW].rearrange("p (a c) -> p a c", c=D)).then_inc(v_hi_done, 1)

            def o_copy(P, g):
                act.wait_ge(pv_done, P * GRP + g + 1)
                if g // 4 == 0:
                    nc.scalar.copy(o_tmp[0:D, :], ps_o[D:P128, 0:GW]).then_inc(o_copy_done, 1)
                else:
                    nc.scalar.copy(o_tmp[D:P128, :], ps_o[0:D, 0:GW]).then_inc(o_copy_done, 1)

            def a_hi_pair(P, p):
                act.wait_ge(mul_done, P + 1)
                if p == 0 and not (isinstance(P, int) and P == 0):
                    act.wait_ge(proj_done, P * 2)
                nc.scalar.copy(a_hi[:, p, :], U[:, p, :]).then_inc(a_hi_done, 1)

            def h_hi_tile(m, k):
                act.wait_ge(h32_done, m * KT + k + 1)
                if k == 0 and not (isinstance(m, int) and m == 0):
                    act.wait_ge(qkv_done, m * PAIRS * CHUNKS)
                nc.scalar.copy(h_hi[:, k, :], x_t[:, k % 2, :]).then_inc(h_hi_done, 1)

            act.wait_ge(const_in, 96)
            for b in range(3 * PAIRS + KT):
                act.wait_ge(w_raw_in[b % 4], 16 * (b // 4 + 1))
                if b >= WSTAGE:
                    act.wait_ge(w_stored[b % WSTAGE], 16 * (b // WSTAGE))
                src = prob[:, (b % 4) // 2, (b % 2) * HALF:(b % 2 + 1) * HALF]
                is_q = b < 3 * PAIRS and b % 3 == 0
                nc.scalar.mul(w_stage(b)[:, 0:HALF], src,
                              SCALE if is_q else 1.0).then_inc(w_hi_done, 1)
            for k in range(KT):
                h_hi_tile(0, k)
            act.wait_ge(bias_done, 1)
            for c in range(CHUNKS):
                qkv32(0, 0, c)
            for piece in range(PIECES):
                v_hi(0, 0, piece)
            exp_tile(0, 0, 0)

            def body(n, has_prev, has_next):
                for q in range(PAIRS * TILES):
                    p, i = q // TILES, q % TILES
                    P = n * PAIRS + p
                    if i + 1 < TILES:
                        exp_tile(P, p % 2, i + 1)
                    elif p < PAIRS - 1 or has_next:
                        exp_tile(P + 1, (p + 1) % 2, i + 1 - TILES)
                    pt_hi_tile(P, i)
                    if (j := vt_at(q - 1, has_next)) is not None:
                        act.wait_ge(vtrans_done, (n * PAIRS + j[0]) * PIECES + j[1] + 1)
                    if has_next and q - 1 in (GN_MEAN_SLOT, GN_VAR_SLOT):
                        act.wait_ge(gavg_done, 2 * (n + 1) + 1 + (GN_MEAN_SLOT, GN_VAR_SLOT).index(q - 1))
                    if i == 1 and (p > 0 or has_prev):
                        act.wait_ge(rtrans_done, P)
                        o_copy(P - 1, GRP - 1)
                    if i >= 3 and i % 2 == 1:
                        o_copy(P, (i - 3) // 2)
                    if (j := vt_at(q - 1, has_next)) is not None:
                        v_hi(n * PAIRS + j[0], j[0] % 2, j[1])
                    if (j := qkv_at(q - 1, has_next)) is not None:
                        qkv32(n * PAIRS + j[0], j[0] % PAIRS, j[1])
                    if (k := found(A_HI_SLOTS, q)) is not None and (k > 0 or has_prev):
                        a_hi_pair(n * PAIRS + k - 1, (k - 1) % PAIRS)
                    if has_next and (k := found(NORM_SLOTS, q - 1)) is not None:
                        h_hi_tile(n + 1, k)

            over_images(act, body)
            last_pair = PAIRS * N_IMG - 1
            act.wait_ge(rtrans_done, last_pair + 1)
            o_copy(last_pair, GRP - 1)
            a_hi_pair(last_pair, PAIRS - 1)

        @block.vector
        def _(dve):
            def as32(ap):
                return ap.bitcast(fp32)

            def max_tile(P, i):
                dve.wait_ge(scores_done, P * TILES + i + 1)
                nc.vector.tensor_reduce(nmax[:, i % 2:i % 2 + 1], ps_s[:, i % 2, :], AX, ALU.max,
                                        negate=True).then_inc(max_done, 1)

            def pt_lo_tile(P, i):
                dve.wait_ge(pt_hi_done, P * TILES + i + 1)
                g = i // 2
                cols = slice((i % 2) * P128, (i % 2 + 1) * P128)
                nc.vector.tensor_tensor(pt_lo[:, g % 2, :, cols], ps_t[:].rearrange("p (t s) -> p t s", s=P128),
                                        as32(pt_hi[:, g % 2, :, cols]), ALU.subtract).then_inc(pt_lo_done, 1)

            def v_lo(P, par, piece):
                dve.wait_ge(v_hi_done, P * PIECES + piece + 1)
                both = V[:, par, 2 * piece:2 * piece + 2].rearrange("p t h c -> p (t h) c")
                nc.vector.tensor_tensor(both[:, :, D:2 * D], ps_o[:, GW:2 * GW].rearrange("p (a c) -> p a c", c=D),
                                        as32(both[:, :, 0:D]), ALU.subtract).then_inc(v_lo_done, 1)

            def o_add(P, p, g):
                dve.wait_ge(o_copy_done, P * GRP + g + 1)
                if g == 0 and not (isinstance(P, int) and P < PAIRS):
                    dve.wait_ge(a_lo_done, P - PAIRS + 1)
                own = slice(0, D) if g // 4 == 0 else slice(D, P128)
                nc.vector.tensor_tensor(U[own, p, (g % 4) * GW:(g % 4 + 1) * GW], ps_o[own, 0:GW], o_tmp[own, :],
                                        ALU.add).then_inc(o_add_done, 1)

            def recip(P, par):
                dve.wait_ge(exp_done, (P + 1) * TILES)
                if not (isinstance(P, int) and P == 0):
                    dve.wait_ge(rtrans_done, P)
                nc.vector.reciprocal(rcp[:], rsum[:, par, :]).then_inc(rcp_done, 1)

            def r_copy(P):
                dve.wait_ge(rtrans_done, P + 1)
                if not (isinstance(P, int) and P == 0):
                    dve.wait_ge(r_out, P * 16)
                    dve.wait_ge(mul_done, P)
                nc.vector.tensor_copy(rT[:], ps_o[0:TILES, GW:GW + P128]).then_inc(rcopy_done, 1)

            steps = [0]

            def link(ins, m, per=24):
                steps[0] += 1
                ins.then_inc(dve_step, 1)
                dve.wait_ge(dve_step, m * per + steps[0])

            GN_LINKS = 3 + 7

            def stats_tile(m, k):
                dve.wait_ge(x_in[k % 2], 16 * (m * KT + k // 2 + 1))
                for half in range(2):
                    ins = nc.vector.bn_stats(bn6[:, k, half, :], x_t[:, k % 2, half * HALF:(half + 1) * HALF])
                ins.then_inc(stat_done, 1)

            parts = bn6[:].rearrange("p k h (e f) -> p (k h e) f", f=3)
            means = parts[:, :, 1].rearrange("p (k e) -> p k e", e=4)

            def channel_means(m):
                dve.wait_ge(stat_done, (m + 1) * KT)
                nc.vector.tensor_reduce(gsum[:], means, AX, ALU.add).then_inc(gn_done, 1)

            def deviations(m):
                dve.wait_ge(gavg_done, 2 * m + 1)
                steps[0] = 0
                nc.vector.tensor_scalar(gmean[:], ps_o[:, GW:GW + KT], 0.25, None, ALU.mult).then_inc(gn_read, 1)
                dve.wait_ge(gn_read, 2 * m + 1)
                every = gmean[:].rearrange("p (k o) -> p k o", o=1).broadcast_to((P128, KT, 4))
                link(nc.vector.tensor_tensor(gdev4[:], means, every, ALU.subtract), m, GN_LINKS)
                flat = gdev4[:].rearrange("p k e -> p (k e)")
                link(nc.vector.tensor_tensor(flat, flat, flat, ALU.mult), m, GN_LINKS)
                link(nc.vector.scalar_tensor_tensor(out=flat, in0=parts[:, :, 2], scalar=4.0 / S, in1=flat,
                                                    op0=ALU.mult, op1=ALU.add), m, GN_LINKS)
                nc.vector.tensor_reduce(gsum[:], gdev4[:], AX, ALU.add).then_inc(gn_done, 1)

            def group_variance(m):
                dve.wait_ge(gavg_done, 2 * m + 2)
                nc.vector.tensor_scalar(gvar[:], ps_o[:, GW:GW + KT], 0.25, EPS, ALU.mult, ALU.add).then_inc(gn_read, 1)

            def coefficients(m):
                dve.wait_ge(root_done, m + 1)
                link(nc.vector.tensor_tensor(gvar[:], gvar[:], grs[:], ALU.mult), m, GN_LINKS)
                link(nc.vector.tensor_tensor(gvar[:], gvar[:], grs[:], ALU.mult), m, GN_LINKS)
                link(nc.vector.tensor_scalar(gvar[:], gvar[:], -0.5, 1.5, ALU.mult, ALU.add), m, GN_LINKS)
                link(nc.vector.tensor_tensor(gvar[:], grs[:], gvar[:], ALU.mult), m, GN_LINKS)
                link(nc.vector.tensor_tensor(gn_a[:], gvar[:], gn_w[:], ALU.mult), m, GN_LINKS)
                link(nc.vector.tensor_tensor(gdev[:], gmean[:], gn_a[:], ALU.mult), m, GN_LINKS)
                link(nc.vector.tensor_tensor(gn_c[:], gn_b[:], gdev[:], ALU.subtract), m, GN_LINKS)

            def h32_tile(m, k):
                dve.wait_ge(x_in[k % 2], 16 * (m * KT + 2 + k // 2 + 1))
                nc.vector.tensor_scalar(x_t[:, k % 2, :], x_t[:, k % 2, :], gn_a[:, k:k + 1], gn_c[:, k:k + 1],
                                        ALU.mult, ALU.add).then_inc(h32_done, 1)

            def proj_out(m, c):
                dve.wait_ge(proj_done, m * PROJ + c + 1)
                dve.wait_ge(res_in[c % RES], 16 * (m * (PROJ // RES) + c // RES + 1))
                nc.vector.scalar_tensor_tensor(out=res[:, c % RES, :], in0=ps_f[:], scalar=b_p[:, c // 2:c // 2 + 1],
                                               in1=res[:, c % RES, :], op0=ALU.add, op1=ALU.add).then_inc(res_done, 1)

            dve.wait_ge(const_in, 96)
            for p in range(PAIRS):
                last = nc.vector.tensor_scalar(b_qkv[:, 3 * p:3 * p + 1], b_qkv[:, 3 * p:3 * p + 1], SCALE, None, ALU.mult)
            last.then_inc(bias_done, 1)

            def w_lo(b):
                dve.wait_ge(w_hi_done, b + 1)
                src = prob[:, (b % 4) // 2, (b % 2) * HALF:(b % 2 + 1) * HALF]
                hi, lo = w_stage(b)[:, 0:HALF], w_stage(b)[:, HALF:]
                is_q = b < 3 * PAIRS and b % 3 == 0
                nc.vector.scalar_tensor_tensor(out=lo, in0=src, scalar=SCALE if is_q else 1.0, in1=as32(hi),
                                               op0=ALU.mult, op1=ALU.subtract).then_inc(w_lo_done, 1)

            for b in range(3 * PAIRS + KT):
                w_lo(b)
                if b % 2 == 1 and b // 2 < KT:
                    stats_tile(0, b // 2)
                if b == 10:
                    channel_means(0)
                    deviations(0)
                    group_variance(0)
                    coefficients(0)
            for k in range(KT):
                h32_tile(0, k)
            for piece in range(PIECES):
                v_lo(0, 0, piece)
            max_tile(0, 0)
            max_tile(0, 1)

            def body(n, has_prev, has_next):
                for q in range(PAIRS * TILES):
                    p, i = q // TILES, q % TILES
                    P = n * PAIRS + p
                    if i == TILES - 1:
                        recip(P, p % 2)
                    if i + 2 < TILES:
                        max_tile(P, i + 2)
                    elif p < PAIRS - 1 or has_next:
                        max_tile(P + 1, i + 2 - TILES)
                    pt_lo_tile(P, i)
                    j = vt_at(q - 1, has_next)
                    if j is not None:
                        dve.wait_ge(v_hi_done, (n * PAIRS + j[0]) * PIECES + j[1] + 1)
                    if i == 1 and (p > 0 or has_prev):
                        o_add(P - 1, (p - 1) % PAIRS, GRP - 1)
                        r_copy(P - 1)
                    if i >= 3 and i % 2 == 1:
                        o_add(P, p, (i - 3) // 2)
                    if j is not None:
                        v_lo(n * PAIRS + j[0], j[0] % 2, j[1])
                    if (c := proj_at(q - 1, has_prev)) is not None:
                        proj_out(n - 1, c)
                    if has_next:
                        if (k := found(STAT_SLOTS, q)) is not None:
                            stats_tile(n + 1, k)
                            if k == KT - 1:
                                channel_means(n + 1)
                        if q == GN_MEAN_SLOT + 1:
                            deviations(n + 1)
                        if q == GN_VAR_SLOT + 1:
                            group_variance(n + 1)
                        if q == GN_VAR_SLOT + 2:
                            coefficients(n + 1)
                        if (k := found(NORM_SLOTS, q)) is not None:
                            h32_tile(n + 1, k)

            over_images(dve, body)
            last_pair = PAIRS * N_IMG - 1
            o_add(last_pair, PAIRS - 1, GRP - 1)
            r_copy(last_pair)
            for c in range(PROJ):
                proj_out(LAST, c)

        @block.gpsimd
        def _(pool):
            def h_lo_tile(m, k):
                pool.wait_ge(h_hi_done, m * KT + k + 1)
                nc.gpsimd.tensor_tensor(h_lo[:, k, :], x_t[:, k % 2, :], h_hi[:, k, :].bitcast(fp32),
                                        ALU.subtract).then_inc(h_lo_done, 1)
                pool.wait_ge(h_lo_done, m * KT + k + 1)

            def split_kq(P, par, c):
                t, half = c // 2, c % 2
                cols = slice(half * HALF, (half + 1) * HALF)
                pool.wait_ge(qkv32_done, P * CHUNKS + c + 1)
                rows = (slice(0, D), slice(D, P128))
                hi = [Q[rows[hd], par, hd, cols] if t == 2 else K[rows[hd], par, hd, 0, cols] for hd in range(2)]
                count = P * 4 + (c if c < 2 else c - 2) + 1
                for hd in range(2):
                    ins = nc.gpsimd.tensor_tensor(hi[hd], kq32[rows[hd], half, :], one[rows[hd], :].broadcast_to((D, HALF)),
                                                  ALU.mult)
                ins.then_inc(kq_hi_done, 1)
                pool.wait_ge(kq_hi_done, count)
                for hd in range(2):
                    lo = kq32[rows[hd], half, :] if t == 2 else K[rows[hd], par, hd, 1, cols]
                    ins = nc.gpsimd.tensor_tensor(lo, kq32[rows[hd], half, :], hi[hd].bitcast(fp32), ALU.subtract)
                ins.then_inc(split_done, 1)
                pool.wait_ge(split_done, count)

            def divide_pair(P, p):
                pool.wait_ge(r_in, (P + 1) * 32)
                pool.wait_ge(o_add_done, (P + 1) * GRP)
                nc.gpsimd.tensor_tensor(U[:, p, :], U[:, p, :], R[:], ALU.mult).then_inc(mul_done, 1)
                pool.wait_ge(mul_done, P + 1)

            def a_lo_pair(P, p):
                pool.wait_ge(a_hi_done, P + 1)
                nc.gpsimd.tensor_tensor(a_lo[:, p, :], U[:, p, :], a_hi[:, p, :].bitcast(fp32),
                                        ALU.subtract).then_inc(a_lo_done, 1)
                pool.wait_ge(a_lo_done, P + 1)

            def root(m):
                pool.wait_ge(gn_read, 2 * m + 2)
                nc.gpsimd.tensor_tensor(grs[:], gvar[:], m_half[:], ALU.pow).then_inc(root_done, 1)
                pool.wait_ge(root_done, m + 1)

            nc.gpsimd.memset(one[:], 1.0)
            nc.gpsimd.memset(m_half[:], -0.5).then_inc(half_set, 1)
            pool.wait_ge(half_set, 1)
            root(0)
            for k in range(KT):
                h_lo_tile(0, k)
            for c in (0, 1, 4, 5):
                split_kq(0, 0, c)

            def body(n, has_prev, has_next):
                for q in range(PAIRS * TILES):
                    p, i = q // TILES, q % TILES
                    P = n * PAIRS + p
                    if has_next and (k := found(NORM_SLOTS, q - 1)) is not None:
                        h_lo_tile(n + 1, k)
                    if (j := qkv_at(q - 1, has_next)) is not None and j[1] not in (2, 3):
                        split_kq(n * PAIRS + j[0], j[0] % 2, j[1])
                    if i == 4 and (p > 0 or has_prev):
                        divide_pair(P - 1, (p - 1) % PAIRS)
                    if (k := found(A_HI_SLOTS, q)) is not None and (k > 0 or has_prev):
                        a_lo_pair(n * PAIRS + k - 1, (k - 1) % PAIRS)
                    if has_next and q == GN_VAR_SLOT + 1:
                        root(n + 1)

            over_images(pool, body)
            divide_pair(PAIRS * N_IMG - 1, PAIRS - 1)
            a_lo_pair(PAIRS * N_IMG - 1, PAIRS - 1)


def kernel(x, L0_conv_norm_w, L0_conv_norm_b, L0_conv_qkv_w, L0_conv_qkv_b, L0_conv_proj_w, L0_conv_proj_b):
    import numpy as np
    import concourse.bacc as bacc
    from concourse.bass_utils import run_bass_kernel_spmd

    x, nw, nb, qw, qb, pw, pb = (np.asarray(a) for a in (
        x, L0_conv_norm_w, L0_conv_norm_b, L0_conv_qkv_w, L0_conv_qkv_b, L0_conv_proj_w, L0_conv_proj_b))
    group = C // 32
    arrays = {
        "x": np.ascontiguousarray(x.reshape(N_IMG, C, S)),
        "wqkvT": np.ascontiguousarray(qw.T),
        "bqkv": np.ascontiguousarray(qb.reshape(3, PAIRS, P128).transpose(2, 1, 0).reshape(P128, 3 * PAIRS)),
        "wpT": np.ascontiguousarray(pw.T),
        "bp": np.ascontiguousarray(pb.reshape(KT, P128).T),
        "gnw": np.ascontiguousarray(nw.reshape(KT, P128).T),
        "gnb": np.ascontiguousarray(nb.reshape(KT, P128).T),
        "ident_in": np.eye(P128, dtype=np.float32),
        "avg_in": np.kron(np.eye(P128 // group, dtype=np.float32), np.full((group, group), 1.0 / group, np.float32)),
    }
    nc = bacc.Bacc("TRN2", target_bir_lowering=False, num_devices=1, dynamic_dma_scratch_size=1024)
    aps = [nc.dram_tensor(n, a.shape, mybir.dt.from_np(a.dtype), kind="ExternalInput").ap() for n, a in arrays.items()]
    out = nc.dram_tensor("out", (N_IMG, C, S), mybir.dt.float32, kind="ExternalOutput").ap()
    build(nc, *aps, out)
    r = run_bass_kernel_spmd(nc, [arrays], core_ids=[0])
    return r.results[0]["out"].reshape(N_IMG, C, 32, 32)
```

```python
from contextlib import ExitStack

import concourse.bass as bass
from concourse import mybir

N_IMG, C, S = 16, 512, 1024
HEADS, D = 8, 64
P128 = 128
KT = C // P128
PAIRS = HEADS // 2
ST = S // P128
TILES = 2 * ST
GRP = 8
GW = 256
HALF = 512
EPS = 1e-5
SCALE = D ** -0.5
CHUNKS = 6
COLUMN = (1, 2, 0)
FIRST = (0, 1, 4, 5, 2, 3)
PIECES = 4
PROJ = 2 * KT
RES = 2
WRING = 2
BLOCKS = 3 * PAIRS + KT
WSTAGE = 8
LAST = N_IMG - 1

QKV_SLOTS = [b + 2 * c for b in (1, 13, 29, 45) for c in range(CHUNKS)]
VT_SLOTS = [b + 7 + 2 * j for b in (1, 13, 29, 45) for j in range(PIECES)]
PROJ_SLOTS = [25, 27, 41, 43, 57, 59, 61, 63]
PROJ_SLOTS_LAST = [25, 27, 41, 43, 45, 47, 49, 51]
STAT_SLOTS = [7, 9, 11, 13]
GN_MEAN_SLOT, GN_VAR_SLOT = 18, 28
NORM_SLOTS = [31, 33, 35, 41]
H_SLOTS = [40, 41, 42, 43]
X_SLOTS = {12: 2, 37: 3}
A_HI_SLOTS = [0, 1, 2, 8]
A_HI_SLOTS_LAST = [53, 55, 57]
PREP_SLOTS = [1, 3, 5, 7, 9, 11, 13, 15]


def found(slots, q):
    return slots.index(q) if q in slots else None


def qkv_at(q, has_next):
    j = found(QKV_SLOTS, q)
    return None if j is None or (j >= 18 and not has_next) else (j // CHUNKS + 1, j % CHUNKS)


def proj_at(q, has_prev, has_next):
    return found(PROJ_SLOTS if has_next else PROJ_SLOTS_LAST, q) if has_prev else None


def a_hi_at(q, has_prev, has_next):
    if has_prev and q in A_HI_SLOTS:
        return A_HI_SLOTS.index(q) - PAIRS
    return None if has_next else found(A_HI_SLOTS_LAST, q)


def vt_at(q, has_next):
    j = found(VT_SLOTS, q)
    return None if j is None or (j >= 12 and not has_next) else (j // PIECES + 1, j % PIECES)


def block_list(has_prev, has_next):
    out = []
    for q in range(PAIRS * TILES):
        if (j := qkv_at(q, has_next)) is not None and j[1] % 2 == 0:
            out.append(("qkv", j[0], j[1] // 2))
        if (c := proj_at(q, has_prev, has_next)) is not None and c % 2 == 0:
            out.append(("proj", c // 2))
    return out


def block_use(n, local):
    if isinstance(n, int) and n == 0:
        return local % WRING, local // WRING + 1
    return local % WRING, n * (BLOCKS // WRING) - KT // WRING + local // WRING + 1


def build(nc, x, wqkvT, bqkv, wpT, bp, gnw, gnb, ident_in, avg_in, out):
    fp32, f32r = mybir.dt.float32, mybir.dt.float32r
    ACT = mybir.ActivationFunctionType
    ALU = mybir.AluOpType
    AX = mybir.AxisListType.X

    w_scr = nc.dram_tensor("w_scr", [3 * PAIRS + KT, P128, 2 * KT * P128], fp32, kind="Internal").ap()
    r_scr = nc.dram_tensor("r_scr", [2, 2, S], fp32, kind="Internal").ap()

    with ExitStack() as ctx:
        def sb(name, shape, dt=fp32):
            return ctx.enter_context(nc.sbuf_tensor(name, shape, dt))

        def sem(name):
            return ctx.enter_context(nc.semaphore(name))

        h_hi = sb("h_hi", [P128, KT, S], f32r)
        h_lo = sb("h_lo", [P128, KT, S], f32r)
        w_ring = sb("w_ring", [P128, WRING, 2, KT, P128], f32r)
        Q = sb("Q", [P128, 2, 2, S], f32r)
        K = sb("K", [P128, 2, 2, 2, S], f32r)
        V = sb("V", [P128, 2, ST, 2, 2 * D], f32r)
        pt_hi = sb("pt_hi", [P128, 2, ST, GW], f32r)
        pt_lo = sb("pt_lo", [P128, 2, ST, GW], f32r)
        prob = sb("prob", [P128, 2, S])
        a_hi = sb("a_hi", [P128, KT, S], f32r)
        a_lo = sb("a_lo", [P128, KT, S], f32r)
        x_t = sb("x_t", [P128, 2, S])
        U = sb("U", [P128, PAIRS, S])
        R = sb("R", [P128, S])
        v32 = sb("v32", [P128, S])
        kq32 = sb("kq32", [P128, 2, HALF])
        o_tmp = sb("o_tmp", [P128, GW])
        res = sb("res", [P128, RES, HALF])
        ident = sb("ident", [P128, P128])
        avg = sb("avg", [P128, P128])
        b_qkv = sb("b_qkv", [P128, 3 * PAIRS])
        b_p = sb("b_p", [P128, KT])
        gn_w = sb("gn_w", [P128, KT])
        gn_b = sb("gn_b", [P128, KT])
        nmax = sb("nmax", [P128, 2])
        rsum = sb("rsum", [P128, 2, TILES])
        rcp = sb("rcp", [P128, TILES])
        rT = sb("rT", [TILES, P128])
        bn6 = sb("bn6", [P128, KT, 2, 6])
        gsum = sb("gsum", [P128, KT])
        gdev4 = sb("gdev4", [P128, KT, 4])
        gmean = sb("gmean", [P128, KT])
        gdev = sb("gdev", [P128, KT])
        gvar = sb("gvar", [P128, KT])
        grs = sb("grs", [P128, KT])
        m_half = sb("m_half", [P128, KT])
        one = sb("one", [P128, 1])
        gn_a = sb("gn_a", [P128, KT])
        gn_c = sb("gn_c", [P128, KT])

        ps_s = ctx.enter_context(nc.psum_tensor("ps_s", [P128, 2, S], fp32))
        ps_t = ctx.enter_context(nc.psum_tensor("ps_t", [P128, S], fp32))
        ps_o = ctx.enter_context(nc.psum_tensor("ps_o", [P128, HALF], fp32))
        ps_f = ctx.enter_context(nc.psum_tensor("ps_f", [P128, HALF], fp32))

        scores_done = sem("scores_done")
        ptrans_done = sem("ptrans_done")
        pv_done = sem("pv_done")
        qkv_done = sem("qkv_done")
        vtrans_done = sem("vtrans_done")
        proj_done = sem("proj_done")
        rtrans_done = sem("rtrans_done")
        gavg_done = sem("gavg_done")
        exp_done = sem("exp_done")
        pt_hi_done = sem("pt_hi_done")
        qkv32_done = sem("qkv32_done")
        v_hi_done = sem("v_hi_done")
        o_copy_done = sem("o_copy_done")
        a_hi_done = sem("a_hi_done")
        h_hi_done = sem("h_hi_done")
        w_hi_done = sem("w_hi_done")
        max_done = sem("max_done")
        pt_lo_done = sem("pt_lo_done")
        v_lo_done = sem("v_lo_done")
        o_add_done = sem("o_add_done")
        rcp_done = sem("rcp_done")
        rcopy_done = sem("rcopy_done")
        stat_done = sem("stat_done")
        gn_read = sem("gn_read")
        gn_done = sem("gn_done")
        h32_done = sem("h32_done")
        res_done = sem("res_done")
        w_lo_done = sem("w_lo_done")
        bias_done = sem("bias_done")
        dve_step = sem("dve_step")
        root_done = sem("root_done")
        kq_hi_done = sem("kq_hi_done")
        split_done = sem("split_done")
        mul_done = sem("mul_done")
        a_lo_done = sem("a_lo_done")
        h_lo_done = sem("h_lo_done")
        half_set = sem("half_set")
        const_in = sem("const_in")
        w_raw_in = [sem(f"w_raw_in{i}") for i in range(WSTAGE)]
        w_stored = [sem(f"w_stored{i}") for i in range(WSTAGE)]
        w_in = [sem(f"w_in{i}") for i in range(WRING)]
        k_copied = sem("k_copied")
        q_moved = [sem(f"q_moved{i}") for i in range(2)]
        x_in = [sem(f"x_in{i}") for i in range(KT)]
        r_out = sem("r_out")
        r_in = sem("r_in")
        res_in = [sem(f"res_in{i}") for i in range(RES)]
        last_w_in = sem("last_w_in")
        last_res_in = [sem(f"last_res_in{i}") for i in range(KT)]
        last_out = sem("last_out")
        res_out = [sem(f"res_out{i}") for i in range(RES)]

        block = ctx.enter_context(nc.Block())
        last_use = BLOCKS * N_IMG - KT - 3

        def over_images(eng, body):
            body(0, False, True)
            with eng.Fori(1, LAST) as n:
                body(n, True, True)
            body(LAST, True, False)

        def w_stage(b):
            return (a_hi, a_lo)[b // KT % 2][:, b % KT, :]

        def ps_t_half(half):
            return ps_t[:, half * HALF:(half + 1) * HALF].rearrange("p (t s) -> p t s", s=P128)

        def pt_half(pt, i, half):
            return pt[:, i // 2 % 2, half * ST // 2:(half + 1) * ST // 2, (i % 2) * P128:(i % 2 + 1) * P128]

        def first_bank(c):
            return ps_s[:, c // 2, c % 2 * HALF:(c % 2 + 1) * HALF] if c < 4 else ps_t[:, (c - 4) * HALF:(c - 3) * HALF]

        def last_bank(c):
            if c < 4:
                return ps_s[:, c // 2, c % 2 * HALF:(c % 2 + 1) * HALF]
            return (ps_t[:, 0:HALF], ps_t[:, HALF:], ps_f[:], ps_o[:])[c - 4]

        def last_res(m):
            return (x_t[:, 0, :], x_t[:, 1, :], v32[:], kq32[:].rearrange("p a s -> p (a s)"))[m]

        def last_w(m, wh, k):
            if m < WRING:
                return w_ring[:, (last_use + m) % WRING, wh, k, :]
            return K[:, 0, m - WRING, wh, k * P128:(k + 1) * P128]

        def w_raw(b):
            place = b if b < 2 else 2 + (b - 2) % 4
            return U[:, place // 2, place % 2 * HALF:(place % 2 + 1) * HALF]

        def w_block(kind):
            return 3 * (kind[1] % PAIRS) + kind[2] if kind[0] == "qkv" else 3 * PAIRS + kind[1]

        def x_home(k):
            return (x_t[:, 0, :], x_t[:, 1, :], U[:, PAIRS - 1, :], R[:])[k]

        def stat_tile(use):
            return (use + 2) % KT

        def x_loads(m, k):
            return 2 * m + 1 if k < 2 else m + 1

        def block_freed(eng, n, kind):
            if kind[0] == "qkv":
                eng.wait_ge(qkv_done, (n * PAIRS + kind[1]) * CHUNKS + 2 * (kind[2] + 1))
            else:
                eng.wait_ge(proj_done, (n - 1) * PROJ + 2 * (kind[1] + 1))

        @block.sync
        def _(sp):
            def load_stat(m, use):
                k = stat_tile(use)
                src = x.rearrange("n c s -> (n c) s")[bass.ds(m * C + k * P128, P128), :]
                if use < 2:
                    sp.wait_ge(h_lo_done, KT * m - KT + use + 1)
                else:
                    sp.wait_ge(stat_done, KT * m + use - 1)
                sp.dma_start(x_t[:, use % 2, :], src).then_inc(x_in[use % 2], 16)

            def load_x(m, k):
                sp.dma_start(x_home(k), x[m, k * P128:(k + 1) * P128, :]).then_inc(x_in[k], 16)

            def load_raw(b):
                if b >= 6:
                    sp.wait_ge(w_lo_done, b - 3)
                if b < 3 * PAIRS:
                    col = COLUMN[b % 3] * C + b // 3 * P128
                    src = wqkvT[:, col:col + P128]
                else:
                    m = b - 3 * PAIRS
                    src = wpT[:, m * P128:(m + 1) * P128]
                sp.dma_start(w_raw(b).rearrange("p (k o) -> p k o", k=KT),
                             src.rearrange("(k p) o -> p k o", p=P128)).then_inc(w_raw_in[b % WSTAGE], 16)

            def store_w(b):
                sp.wait_ge(w_hi_done, b + 1)
                sp.wait_ge(w_lo_done, b + 1)
                sp.dma_start(w_scr[b], w_stage(b).bitcast(fp32)).then_inc(w_stored[b % WSTAGE], 16)

            def load_w(b, slot):
                sp.dma_start(w_ring[:, slot].rearrange("p a k o -> p (a k o)").bitcast(fp32), w_scr[b]).then_inc(w_in[slot], 16)

            def copy_k(P, par, half):
                sp.wait_ge(split_done, P * 4 + 1 + half)
                cols = slice(half * HALF, (half + 1) * HALF)
                sp.dma_start(K[D:P128, par, 0, :, cols].bitcast(fp32), K[0:D, par, 0, :, cols].bitcast(fp32)).then_inc(k_copied, 16)
                sp.dma_start(K[0:D, par, 1, :, cols].bitcast(fp32), K[D:P128, par, 1, :, cols].bitcast(fp32)).then_inc(k_copied, 16)

            def move_q(P, par, half):
                sp.wait_ge(split_done, P * 4 + 3 + half)
                cols = slice(half * HALF, (half + 1) * HALF)
                sp.dma_start(Q[D:P128, par, 0, cols].bitcast(fp32), kq32[0:D, half, :]).then_inc(q_moved[half], 16)
                sp.dma_start(Q[0:D, par, 1, cols].bitcast(fp32), kq32[D:P128, half, :]).then_inc(q_moved[half], 16)

            def spread_r(P, par):
                sp.wait_ge(rcopy_done, P + 1)
                sp.dma_start(r_scr[par].rearrange("h (t s) -> (h t) s", s=P128), rT[:]).then_inc(r_out, 16)
                sp.wait_ge(r_out, (P + 1) * 16)
                sp.dma_start(R[0:D, :], r_scr[par, 0:1, :].broadcast_to((D, S))).then_inc(r_in, 16)
                sp.dma_start(R[D:P128, :], r_scr[par, 1:2, :].broadcast_to((D, S))).then_inc(r_in, 16)

            def res_use(m, c):
                return c % RES, m * (PROJ // RES) + c // RES + 1

            def load_res(m, c):
                s, uses = res_use(m, c)
                if c >= RES:
                    sp.wait_ge(res_out[s], (uses - 1) * 16)
                mt, half = c // 2, c % 2
                sp.dma_start(res[:, s, :], x[m, mt * P128:(mt + 1) * P128, half * HALF:(half + 1) * HALF]
                             ).then_inc(res_in[s], 16)

            def store_res(m, c):
                s, _ = res_use(m, c)
                mt, half = c // 2, c % 2
                sp.wait_ge(res_done, m * PROJ + c + 1)
                sp.dma_start(out[m, mt * P128:(mt + 1) * P128, half * HALF:(half + 1) * HALF], res[:, s, :]
                             ).then_inc(res_out[s], 16)

            for k in range(KT):
                load_x(0, k)
            sp.dma_start(ident[:], ident_in).then_inc(const_in, 16)
            sp.dma_start(avg[:], avg_in).then_inc(const_in, 16)
            sp.dma_start(b_qkv[:], bqkv).then_inc(const_in, 16)
            sp.dma_start(b_p[:], bp).then_inc(const_in, 16)
            sp.dma_start(gn_w[:], gnw).then_inc(const_in, 16)
            sp.dma_start(gn_b[:], gnb).then_inc(const_in, 16)
            for b in range(6):
                load_raw(b)
            for b in range(WSTAGE):
                store_w(b)
                if b + 6 < WSTAGE:
                    load_raw(b + 6)
            for t in range(WRING):
                b = w_block(("qkv", 1, t))
                sp.wait_ge(w_stored[b], 16)
                load_w(b, t)
            for half in range(2):
                copy_k(0, 0, half)
            for half in range(2):
                move_q(0, 0, half)

            def body(n, has_prev, has_next):
                blocks = block_list(has_prev, has_next)
                following = ([("qkv", 1, 0), ("qkv", 1, 1)] if has_next else [("proj", 0), ("proj", 1)])
                blocks_from = blocks + following

                def load_after(local):
                    block_freed(sp, n, blocks[local])
                    nxt = local + WRING
                    if nxt < len(blocks):
                        slot = block_use(n, nxt)[0]
                    elif has_next:
                        slot = block_use(n + 1, nxt - len(blocks))[0]
                    else:
                        slot = (last_use + nxt - len(blocks)) % WRING
                    b = w_block(blocks_from[nxt])
                    if not has_prev:
                        sp.wait_ge(w_stored[b % WSTAGE], 16 * (b // WSTAGE + 1))
                    load_w(b, slot)

                for q in range(PAIRS * TILES):
                    p, i = q // TILES, q % TILES
                    P = n * PAIRS + p
                    if not has_prev and (k := found(PREP_SLOTS, q)) is not None:
                        load_raw(WSTAGE + k)
                    if not has_prev and (k := found(PREP_SLOTS, q - 2)) is not None:
                        store_w(WSTAGE + k)
                    if i == 2 and (p > 0 or has_prev):
                        spread_r(P - 1, (p - 1) % 2)
                    if (j := qkv_at(q - 1, has_next)) is not None and j[1] % 2 == 1:
                        load_after(blocks.index(("qkv", j[0], j[1] // 2)))
                    if (c := proj_at(q - 1, has_prev, has_next)) is not None and c % 2 == 1:
                        load_after(blocks.index(("proj", c // 2)))
                    if (j := qkv_at(q - 2, has_next)) is not None:
                        if j[1] < 2:
                            copy_k(n * PAIRS + j[0], j[0] % 2, j[1])
                        elif j[1] >= 4:
                            move_q(n * PAIRS + j[0], j[0] % 2, j[1] - 4)
                    if (c := proj_at(q - 2, has_prev, has_next)) is not None:
                        store_res(n - 1, c)
                    if (c := proj_at(q + 1, has_prev, has_next)) is not None:
                        load_res(n - 1, c)
                    if has_next:
                        if (k := found(STAT_SLOTS, q + 1)) is not None:
                            load_stat(n + 1, k)
                        if q in X_SLOTS:
                            if X_SLOTS[q] == 3:
                                sp.wait_ge(mul_done, n * PAIRS + 2)
                            elif has_prev:
                                sp.wait_ge(a_lo_done, n * PAIRS)
                            else:
                                sp.wait_ge(h_lo_done, KT)
                            load_x(n + 1, X_SLOTS[q])
                if has_prev and has_next:
                    store_res(n - 1, PROJ - 1)
                    results = n * (16 * PROJ // RES)
                    for s in range(RES):
                        sp.wait_ge(res_out[s], results)
                    load_after(blocks.index(("proj", KT - 1)))

            over_images(sp, body)
            sp.wait_ge(scores_done, (PAIRS * N_IMG - 1) * TILES)
            for m in range(WRING, KT):
                w = w_scr[3 * PAIRS + m].rearrange("p (a s) -> p a s", a=2)
                sp.dma_start(K[:, 0, m - WRING, :, 0:HALF].bitcast(fp32), w).then_inc(last_w_in, 16)
            sp.wait_ge(h_lo_done, KT * N_IMG)
            sp.wait_ge(v_lo_done, PAIRS * N_IMG * PIECES)
            sp.wait_ge(q_moved[0], PAIRS * N_IMG * 32)
            sp.wait_ge(q_moved[1], PAIRS * N_IMG * 32)
            for m in range(KT):
                sp.dma_start(last_res(m), x[LAST, m * P128:(m + 1) * P128, :]).then_inc(last_res_in[m], 16)
            spread_r(PAIRS * N_IMG - 1, 1)
            sp.wait_ge(res_out[0], LAST * (16 * PROJ // RES))
            sp.wait_ge(res_out[1], LAST * (16 * PROJ // RES))
            for c in range(PROJ):
                m, half = c // 2, c % 2
                cols = slice(half * HALF, (half + 1) * HALF)
                sp.wait_ge(res_done, LAST * PROJ + c + 1)
                sp.dma_start(out[LAST, m * P128:(m + 1) * P128, cols], last_res(m)[:, cols]).then_inc(last_out, 16)
            sp.wait_ge(last_out, 16 * PROJ)

        @block.tensor
        def _(pe):
            o_free = [None]
            fill_free = [None]

            def take_fill_bank(freed_by):
                if fill_free[0] is not None:
                    pe.wait_ge(*fill_free[0])
                fill_free[0] = freed_by

            def in_ring(w):
                return lambda wh, k: w_ring[:, w, wh, k, :]

            def in_stage(b):
                return lambda wh, k: w_stage(b)[:, wh * HALF + k * P128:wh * HALF + (k + 1) * P128]

            def three_passes(w, hi, lo, cols, bank=ps_f[:]):
                steps = [(k, wh, mov) for k in range(KT) for wh, mov in ((0, hi), (0, lo), (1, hi))]
                for j, (k, wh, mov) in enumerate(steps):
                    last = nc.tensor.matmul(bank, w(wh, k), mov[:, k, cols], start=(j == 0), stop=(j == len(steps) - 1))
                return last

            def first_chunk(j):
                b, half = FIRST[j] // 2, FIRST[j] % 2
                pe.wait_ge(w_hi_done, b + 1)
                pe.wait_ge(w_lo_done, b + 1)
                three_passes(in_stage(b), h_hi, h_lo, slice(half * HALF, (half + 1) * HALF), first_bank(j)
                             ).then_inc(qkv_done, 1)

            def qkv_chunk(P, c, ring, loads):
                if c % 2 == 0:
                    pe.wait_ge(w_in[ring], loads * 16)
                half = c % 2
                take_fill_bank((qkv32_done, P * CHUNKS + c + 1))
                three_passes(in_ring(ring), h_hi, h_lo, slice(half * HALF, (half + 1) * HALF)).then_inc(qkv_done, 1)

            def h_ready(m):
                pe.wait_ge(h_hi_done, (m + 1) * KT)
                pe.wait_ge(h_lo_done, (m + 1) * KT)

            def proj_chunk(m, c, ring, loads):
                if c == 0:
                    pe.wait_ge(a_hi_done, (m + 1) * PAIRS)
                    pe.wait_ge(a_lo_done, (m + 1) * PAIRS)
                if c % 2 == 0:
                    pe.wait_ge(w_in[ring], loads * 16)
                half = c % 2
                take_fill_bank((res_done, m * PROJ + c + 1))
                three_passes(in_ring(ring), a_hi, a_lo, slice(half * HALF, (half + 1) * HALF)).then_inc(proj_done, 1)

            def group_average(m, step):
                pe.wait_ge(gn_done, 2 * m + 1 + step)
                o_free[0] = (gn_read, 2 * m + 1 + step)
                nc.tensor.matmul(ps_o[:, GW:GW + KT], avg[:], gsum[:], start=True, stop=True).then_inc(gavg_done, 1)

            def transpose_v(P, piece):
                pe.wait_ge(qkv32_done, P * CHUNKS + 3 + piece // 2)
                o_free[0] = (v_lo_done, P * PIECES + piece + 1)
                for j in range(2):
                    t = 2 * piece + j
                    last = nc.tensor.transpose(ps_o[:, GW + j * P128:GW + (j + 1) * P128], v32[:, t * P128:(t + 1) * P128], ident[:])
                last.then_inc(vtrans_done, 1)

            def transpose_p(P, i):
                for half in range(2):
                    if i > 0 or not (isinstance(P, int) and P == 0):
                        pe.wait_ge(pt_lo_done, 2 * (P * TILES + i) - 1 + half)
                    for t in range(half * ST // 2, (half + 1) * ST // 2):
                        cols = slice(t * P128, (t + 1) * P128)
                        last = nc.tensor.transpose(ps_t[:, cols], prob[:, i % 2, cols], ident[:])
                    last.then_inc(ptrans_done, 1)

            def scores(P, par, i):
                if i == 0:
                    pe.wait_ge(k_copied, (P + 1) * 64)
                    pe.wait_ge(q_moved[0], (P + 1) * 32)
                if i == ST // 2:
                    pe.wait_ge(q_moved[1], (P + 1) * 32)
                hd, t = i // ST, i % ST
                for half in range(2):
                    for hl in range(2):
                        last = nc.tensor.matmul(ps_s[:, i % 2, half * HALF:(half + 1) * HALF],
                                                Q[:, par, hd, t * P128:(t + 1) * P128],
                                                K[:, par, hd, hl, half * HALF:(half + 1) * HALF],
                                                start=(hl == 0), stop=(hl == 1))
                last.then_inc(scores_done, 1)

            def pv_group(P, par, g):
                pe.wait_ge(pt_lo_done, 2 * (P * TILES + 2 * g + 2))
                if g == 0:
                    pe.wait_ge(v_lo_done, (P + 1) * PIECES)
                if o_free[0] is not None:
                    pe.wait_ge(*o_free[0])
                    o_free[0] = None
                if g > 0 or not (isinstance(P, int) and P == 0):
                    pe.wait_ge(o_add_done, P * GRP + g)
                for t in range(ST):
                    for j, pt in enumerate((pt_hi, pt_lo)):
                        last = nc.tensor.matmul(ps_o[:, 0:GW], V[:, par, t, g // 4, :], pt[:, g % 2, t, :],
                                                start=(t == 0 and j == 0), stop=(t == ST - 1 and j == 1))
                last.then_inc(pv_done, 1)

            def transpose_r(P):
                pe.wait_ge(rcp_done, P + 1)
                o_free[0] = (rcopy_done, P + 1)
                nc.tensor.transpose(ps_o[0:TILES, GW:GW + P128], rcp[:], ident[:]).then_inc(rtrans_done, 1)

            pe.wait_ge(const_in, 96)
            group_average(0, 0)
            pe.wait_ge(gn_read, 1)
            group_average(0, 1)
            pe.wait_ge(gn_read, 2)
            h_ready(0)
            for j in range(CHUNKS):
                first_chunk(j)
            pe.wait_ge(qkv32_done, CHUNKS)
            transpose_v(0, 0)
            scores(0, 0, 0)
            pe.wait_ge(v_lo_done, 1)
            transpose_v(0, 1)
            scores(0, 0, 1)
            for piece in (2, 3):
                pe.wait_ge(v_lo_done, piece)
                transpose_v(0, piece)

            def body(n, has_prev, has_next):
                fill_free[0] = None
                o_free[0] = (v_lo_done, (n * PAIRS + 1) * PIECES)
                blocks = block_list(has_prev, has_next)
                for q in range(PAIRS * TILES):
                    p, i = q // TILES, q % TILES
                    P = n * PAIRS + p
                    pe.wait_ge(exp_done, P * TILES + i + 1)
                    if i + 2 < TILES:
                        scores(P, p % 2, i + 2)
                    elif p < PAIRS - 1 or has_next:
                        scores(P + 1, (p + 1) % 2, i + 2 - TILES)
                    transpose_p(P, i)
                    if i == 0 and (p > 0 or has_prev):
                        pv_group(P - 1, (p - 1) % 2, GRP - 1)
                        transpose_r(P - 1)
                    if i > 0 and i % 2 == 0:
                        pv_group(P, p % 2, i // 2 - 1)
                    if has_next and q in (GN_MEAN_SLOT, GN_VAR_SLOT):
                        group_average(n + 1, (GN_MEAN_SLOT, GN_VAR_SLOT).index(q))
                    if (j := vt_at(q, has_next)) is not None:
                        transpose_v(n * PAIRS + j[0], j[1])
                    if (j := qkv_at(q, has_next)) is not None:
                        if j == (PAIRS, 0):
                            h_ready(n + 1)
                        qkv_chunk(n * PAIRS + j[0], j[1], *block_use(n, blocks.index(("qkv", j[0], j[1] // 2))))
                    if (c := proj_at(q, has_prev, has_next)) is not None:
                        proj_chunk(n - 1, c, *block_use(n, blocks.index(("proj", c // 2))))

            over_images(pe, body)
            last_pair = PAIRS * N_IMG - 1
            pv_group(last_pair, (PAIRS - 1) % 2, GRP - 1)
            transpose_r(last_pair)

            def last_projection(c, k):
                cols = slice(c % 2 * HALF, (c % 2 + 1) * HALF)
                for wh, mov in ((0, a_hi), (0, a_lo), (1, a_hi)):
                    last = nc.tensor.matmul(last_bank(c), last_w(c // 2, wh, k), mov[:, k, cols],
                                            start=(k == 0 and wh == 0 and mov is a_hi), stop=(k == KT - 1 and wh == 1))
                return last

            pe.wait_ge(a_hi_done, last_pair)
            pe.wait_ge(a_lo_done, last_pair)
            pe.wait_ge(res_done, LAST * PROJ)
            pe.wait_ge(w_in[last_use % WRING], (last_use // WRING + 1) * 16)
            pe.wait_ge(w_in[(last_use + 1) % WRING], ((last_use + 1) // WRING + 1) * 16)
            pe.wait_ge(last_w_in, 32)
            for c in range(PROJ):
                if c == PROJ - 1:
                    pe.wait_ge(o_add_done, PAIRS * N_IMG * GRP)
                    pe.wait_ge(rcopy_done, PAIRS * N_IMG)
                for k in range(KT - 1):
                    last_projection(c, k)
            pe.wait_ge(a_hi_done, last_pair + 1)
            pe.wait_ge(a_lo_done, last_pair + 1)
            for c in range(PROJ):
                last_projection(c, KT - 1).then_inc(proj_done, 1)

        @block.scalar
        def _(act):
            def exp_tile(P, par, i):
                act.wait_ge(max_done, P * TILES + i + 1)
                if i == 0 and not (isinstance(P, int) and P < 2):
                    act.wait_ge(rcp_done, P - 1)
                nc.scalar.activation(prob[:, i % 2, :], ps_s[:, i % 2, :], ACT.Exp, bias=nmax[:, i % 2:i % 2 + 1],
                                     accum_out=rsum[:, par, i:i + 1]).then_inc(exp_done, 1)

            def pt_hi_tile(P, i):
                g = i // 2
                for half in range(2):
                    act.wait_ge(ptrans_done, 2 * (P * TILES + i) + 1 + half)
                    if half == 0 and i % 2 == 0 and (g >= 2 or not (isinstance(P, int) and P == 0)):
                        act.wait_ge(pv_done, P * GRP + g - 1)
                    nc.scalar.copy(pt_half(pt_hi, i, half), ps_t_half(half)).then_inc(pt_hi_done, 1)

            def qkv32(P, p, c, bank=ps_f[:], count=None):
                t, half = c // 2, c % 2
                cols = slice(half * HALF, (half + 1) * HALF)
                b = 3 * p + COLUMN[t]
                act.wait_ge(qkv_done, P * CHUNKS + c + 1 if count is None else count)
                if t == 0 and not (isinstance(P, int) and P == 0):
                    act.wait_ge(q_moved[half], P * 32)
                if t == 2:
                    act.wait_ge(split_done, P * 4 + 1 + half)
                nc.scalar.activation(v32[:, cols] if t == 1 else kq32[:, half, :], bank, ACT.Identity,
                                     bias=b_qkv[:, b:b + 1]).then_inc(qkv32_done, 1)

            def v_hi(P, par, piece):
                act.wait_ge(vtrans_done, P * PIECES + piece + 1)
                dst = V[:, par, 2 * piece:2 * piece + 2].rearrange("p t h c -> p (t h) c")[:, :, 0:D]
                nc.scalar.copy(dst, ps_o[:, GW:2 * GW].rearrange("p (a c) -> p a c", c=D)).then_inc(v_hi_done, 1)

            def o_copy(P, g):
                act.wait_ge(pv_done, P * GRP + g + 1)
                if g // 4 == 0:
                    nc.scalar.copy(o_tmp[0:D, :], ps_o[D:P128, 0:GW]).then_inc(o_copy_done, 1)
                else:
                    nc.scalar.copy(o_tmp[D:P128, :], ps_o[0:D, 0:GW]).then_inc(o_copy_done, 1)

            def a_hi_pair(P, p):
                act.wait_ge(mul_done, P + 1)
                nc.scalar.copy(a_hi[:, p, :], U[:, p, :]).then_inc(a_hi_done, 1)

            def h_hi_tile(m, k):
                act.wait_ge(h32_done, m * KT + k + 1)
                if k == 0 and not (isinstance(m, int) and m == 0):
                    act.wait_ge(qkv_done, m * PAIRS * CHUNKS)
                nc.scalar.copy(h_hi[:, k, :], x_home(k)).then_inc(h_hi_done, 1)

            def w_hi(b):
                act.wait_ge(w_raw_in[b % WSTAGE], 16 * (b // WSTAGE + 1))
                if b >= WSTAGE:
                    act.wait_ge(w_stored[b % WSTAGE], 16 * (b // WSTAGE))
                if WSTAGE <= b < WSTAGE + 3:
                    act.wait_ge(qkv_done, CHUNKS)
                is_q = b < 3 * PAIRS and b % 3 == 2
                nc.scalar.mul(w_stage(b)[:, 0:HALF], w_raw(b), SCALE if is_q else 1.0
                              ).then_inc(w_hi_done, 1)

            for b in range(3):
                w_hi(b)
            for k in range(KT):
                h_hi_tile(0, k)
            for b in range(3, WSTAGE):
                w_hi(b)
            act.wait_ge(bias_done, 1)
            for j in range(CHUNKS):
                qkv32(0, 0, FIRST[j], first_bank(j), j + 1)
            v_hi(0, 0, 0)
            v_hi(0, 0, 1)
            exp_tile(0, 0, 0)
            v_hi(0, 0, 2)
            v_hi(0, 0, 3)

            def body(n, has_prev, has_next):
                for q in range(PAIRS * TILES):
                    p, i = q // TILES, q % TILES
                    P = n * PAIRS + p
                    if i + 1 < TILES:
                        exp_tile(P, p % 2, i + 1)
                    elif p < PAIRS - 1 or has_next:
                        exp_tile(P + 1, (p + 1) % 2, i + 1 - TILES)
                    pt_hi_tile(P, i)
                    if (j := vt_at(q - 1, has_next)) is not None:
                        act.wait_ge(vtrans_done, (n * PAIRS + j[0]) * PIECES + j[1] + 1)
                    if has_next and q - 1 in (GN_MEAN_SLOT, GN_VAR_SLOT):
                        act.wait_ge(gavg_done, 2 * (n + 1) + 1 + (GN_MEAN_SLOT, GN_VAR_SLOT).index(q - 1))
                    if i == 1 and (p > 0 or has_prev):
                        act.wait_ge(rtrans_done, P)
                        o_copy(P - 1, GRP - 1)
                    if i >= 3 and i % 2 == 1:
                        o_copy(P, (i - 3) // 2)
                    if (j := vt_at(q - 1, has_next)) is not None:
                        v_hi(n * PAIRS + j[0], j[0] % 2, j[1])
                    if (j := qkv_at(q - 1, has_next)) is not None:
                        qkv32(n * PAIRS + j[0], j[0] % PAIRS, j[1])
                    if (j := a_hi_at(q, has_prev, has_next)) is not None:
                        a_hi_pair(n * PAIRS + j, j % PAIRS)
                    if has_next and (k := found(H_SLOTS, q)) is not None:
                        h_hi_tile(n + 1, k)
                    if not has_prev and (k := found(PREP_SLOTS, q - 1)) is not None:
                        w_hi(WSTAGE + k)
                if not has_prev:
                    for s in range(WSTAGE):
                        act.wait_ge(w_stored[s], 16 * BLOCKS // WSTAGE)

            over_images(act, body)
            last_pair = PAIRS * N_IMG - 1
            act.wait_ge(rtrans_done, last_pair + 1)
            o_copy(last_pair, GRP - 1)
            a_hi_pair(last_pair, PAIRS - 1)

        @block.vector
        def _(dve):
            def as32(ap):
                return ap.bitcast(fp32)

            def max_tile(P, i):
                dve.wait_ge(scores_done, P * TILES + i + 1)
                nc.vector.tensor_reduce(nmax[:, i % 2:i % 2 + 1], ps_s[:, i % 2, :], AX, ALU.max,
                                        negate=True).then_inc(max_done, 1)

            def pt_lo_tile(P, i):
                for half in range(2):
                    dve.wait_ge(pt_hi_done, 2 * (P * TILES + i) + 1 + half)
                    nc.vector.tensor_tensor(pt_half(pt_lo, i, half), ps_t_half(half), as32(pt_half(pt_hi, i, half)),
                                            ALU.subtract).then_inc(pt_lo_done, 1)

            def v_lo(P, par, piece):
                dve.wait_ge(v_hi_done, P * PIECES + piece + 1)
                both = V[:, par, 2 * piece:2 * piece + 2].rearrange("p t h c -> p (t h) c")
                nc.vector.tensor_tensor(both[:, :, D:2 * D], ps_o[:, GW:2 * GW].rearrange("p (a c) -> p a c", c=D),
                                        as32(both[:, :, 0:D]), ALU.subtract).then_inc(v_lo_done, 1)

            def o_add(P, p, g):
                dve.wait_ge(o_copy_done, P * GRP + g + 1)
                if g == 0 and not (isinstance(P, int) and P < PAIRS):
                    dve.wait_ge(a_lo_done, P - PAIRS + 1)
                own = slice(0, D) if g // 4 == 0 else slice(D, P128)
                nc.vector.tensor_tensor(U[own, p, (g % 4) * GW:(g % 4 + 1) * GW], ps_o[own, 0:GW], o_tmp[own, :],
                                        ALU.add).then_inc(o_add_done, 1)

            def recip(P, par):
                dve.wait_ge(exp_done, (P + 1) * TILES)
                if not (isinstance(P, int) and P == 0):
                    dve.wait_ge(rtrans_done, P)
                nc.vector.reciprocal(rcp[:], rsum[:, par, :]).then_inc(rcp_done, 1)

            def r_copy(P):
                dve.wait_ge(rtrans_done, P + 1)
                if not (isinstance(P, int) and P == 0):
                    dve.wait_ge(r_out, P * 16)
                    dve.wait_ge(mul_done, P)
                nc.vector.tensor_copy(rT[:], ps_o[0:TILES, GW:GW + P128]).then_inc(rcopy_done, 1)

            steps = [0]

            def link(ins, m, per):
                steps[0] += 1
                ins.then_inc(dve_step, 1)
                dve.wait_ge(dve_step, m * per + steps[0])

            GN_LINKS = 3 + 7

            def stats_tile(k, src):
                for half in range(2):
                    ins = nc.vector.bn_stats(bn6[:, k, half, :], src[:, half * HALF:(half + 1) * HALF])
                ins.then_inc(stat_done, 1)

            parts = bn6[:].rearrange("p k h (e f) -> p (k h e) f", f=3)
            means = parts[:, :, 1].rearrange("p (k e) -> p k e", e=4)

            def channel_means(m):
                dve.wait_ge(stat_done, (m + 1) * KT)
                nc.vector.tensor_reduce(gsum[:], means, AX, ALU.add).then_inc(gn_done, 1)

            def deviations(m):
                dve.wait_ge(gavg_done, 2 * m + 1)
                steps[0] = 0
                nc.vector.tensor_scalar(gmean[:], ps_o[:, GW:GW + KT], 0.25, None, ALU.mult).then_inc(gn_read, 1)
                dve.wait_ge(gn_read, 2 * m + 1)
                every = gmean[:].rearrange("p (k o) -> p k o", o=1).broadcast_to((P128, KT, 4))
                link(nc.vector.tensor_tensor(gdev4[:], means, every, ALU.subtract), m, GN_LINKS)
                flat = gdev4[:].rearrange("p k e -> p (k e)")
                link(nc.vector.tensor_tensor(flat, flat, flat, ALU.mult), m, GN_LINKS)
                link(nc.vector.scalar_tensor_tensor(out=flat, in0=parts[:, :, 2], scalar=4.0 / S, in1=flat,
                                                    op0=ALU.mult, op1=ALU.add), m, GN_LINKS)
                nc.vector.tensor_reduce(gsum[:], gdev4[:], AX, ALU.add).then_inc(gn_done, 1)

            def group_variance(m):
                dve.wait_ge(gavg_done, 2 * m + 2)
                nc.vector.tensor_scalar(gvar[:], ps_o[:, GW:GW + KT], 0.25, EPS, ALU.mult, ALU.add).then_inc(gn_read, 1)

            def coefficients(m):
                dve.wait_ge(root_done, m + 1)
                link(nc.vector.tensor_tensor(gvar[:], gvar[:], grs[:], ALU.mult), m, GN_LINKS)
                link(nc.vector.tensor_tensor(gvar[:], gvar[:], grs[:], ALU.mult), m, GN_LINKS)
                link(nc.vector.tensor_scalar(gvar[:], gvar[:], -0.5, 1.5, ALU.mult, ALU.add), m, GN_LINKS)
                link(nc.vector.tensor_tensor(gvar[:], grs[:], gvar[:], ALU.mult), m, GN_LINKS)
                link(nc.vector.tensor_tensor(gn_a[:], gvar[:], gn_w[:], ALU.mult), m, GN_LINKS)
                link(nc.vector.tensor_tensor(gdev[:], gmean[:], gn_a[:], ALU.mult), m, GN_LINKS)
                link(nc.vector.tensor_tensor(gn_c[:], gn_b[:], gdev[:], ALU.subtract), m, GN_LINKS)

            def h32_tile(m, k):
                dve.wait_ge(x_in[k], 16 * x_loads(m, k))
                nc.vector.tensor_scalar(x_home(k), x_home(k), gn_a[:, k:k + 1], gn_c[:, k:k + 1],
                                        ALU.mult, ALU.add).then_inc(h32_done, 1)

            def proj_out(m, c):
                dve.wait_ge(proj_done, m * PROJ + c + 1)
                dve.wait_ge(res_in[c % RES], 16 * (m * (PROJ // RES) + c // RES + 1))
                nc.vector.scalar_tensor_tensor(out=res[:, c % RES, :], in0=ps_f[:], scalar=b_p[:, c // 2:c // 2 + 1],
                                               in1=res[:, c % RES, :], op0=ALU.add, op1=ALU.add).then_inc(res_done, 1)

            def w_lo(b):
                dve.wait_ge(w_hi_done, b + 1)
                hi, lo = w_stage(b)[:, 0:HALF], w_stage(b)[:, HALF:]
                is_q = b < 3 * PAIRS and b % 3 == 2
                nc.vector.scalar_tensor_tensor(out=lo, in0=w_raw(b), scalar=SCALE if is_q else 1.0, in1=as32(hi),
                                               op0=ALU.mult, op1=ALU.subtract).then_inc(w_lo_done, 1)

            def h_lo_first(k):
                dve.wait_ge(h_hi_done, k + 1)
                nc.vector.tensor_tensor(h_lo[:, k, :], x_home(k), as32(h_hi[:, k, :]), ALU.subtract).then_inc(h_lo_done, 1)

            for k in range(KT):
                dve.wait_ge(x_in[k], 16)
                stats_tile(k, x_home(k))
            channel_means(0)
            dve.wait_ge(const_in, 96)
            for p in range(PAIRS):
                last = nc.vector.tensor_scalar(b_qkv[:, 3 * p:3 * p + 1], b_qkv[:, 3 * p:3 * p + 1], SCALE, None, ALU.mult)
            last.then_inc(bias_done, 1)
            deviations(0)
            group_variance(0)
            for b in range(3):
                w_lo(b)
            coefficients(0)
            for k in range(KT):
                h32_tile(0, k)
                if k > 0:
                    h_lo_first(k - 1)
            h_lo_first(KT - 1)
            for b in range(3, WSTAGE):
                w_lo(b)
            for half in range(2):
                dve.wait_ge(qkv32_done, half + 1)
                cols = slice(half * HALF, (half + 1) * HALF)
                rows = (slice(0, D), slice(D, P128))
                for hd in range(2):
                    last = nc.vector.tensor_copy(K[rows[hd], 0, hd, 0, cols], kq32[rows[hd], half, :])
                last.then_inc(kq_hi_done, 1)
                dve.wait_ge(kq_hi_done, half + 1)
                for hd in range(2):
                    last = nc.vector.tensor_tensor(K[rows[hd], 0, hd, 1, cols], kq32[rows[hd], half, :],
                                                   as32(K[rows[hd], 0, hd, 0, cols]), ALU.subtract)
                last.then_inc(split_done, 1)
            v_lo(0, 0, 0)
            max_tile(0, 0)
            v_lo(0, 0, 1)
            max_tile(0, 1)
            v_lo(0, 0, 2)
            v_lo(0, 0, 3)

            def body(n, has_prev, has_next):
                for q in range(PAIRS * TILES):
                    p, i = q // TILES, q % TILES
                    P = n * PAIRS + p
                    if i == TILES - 1:
                        recip(P, p % 2)
                    if i + 2 < TILES:
                        max_tile(P, i + 2)
                    elif p < PAIRS - 1 or has_next:
                        max_tile(P + 1, i + 2 - TILES)
                    pt_lo_tile(P, i)
                    j = vt_at(q - 1, has_next)
                    if j is not None:
                        dve.wait_ge(v_hi_done, (n * PAIRS + j[0]) * PIECES + j[1] + 1)
                    if i == 1 and (p > 0 or has_prev):
                        o_add(P - 1, (p - 1) % PAIRS, GRP - 1)
                        if not has_prev and p == 1:
                            dve.wait_ge(h_lo_done, KT)
                        if has_next and p == PAIRS - 1:
                            dve.wait_ge(h_lo_done, KT * (n + 2))
                        r_copy(P - 1)
                    if i >= 3 and i % 2 == 1:
                        if has_next and p == PAIRS - 1 and i == 3:
                            dve.wait_ge(h_lo_done, KT * (n + 2))
                        o_add(P, p, (i - 3) // 2)
                    if j is not None:
                        v_lo(n * PAIRS + j[0], j[0] % 2, j[1])
                    if (c := proj_at(q - 1, has_prev, has_next)) is not None:
                        proj_out(n - 1, c)
                    if has_next:
                        if (k := found(STAT_SLOTS, q)) is not None:
                            dve.wait_ge(x_in[k % 2], 16 * (2 * (n + 1) + k // 2))
                            stats_tile(stat_tile(k), x_t[:, k % 2, :])
                            if k == KT - 1:
                                channel_means(n + 1)
                        if q == GN_MEAN_SLOT + 1:
                            deviations(n + 1)
                        if q == GN_VAR_SLOT + 1:
                            group_variance(n + 1)
                        if q == GN_VAR_SLOT + 2:
                            coefficients(n + 1)
                        if (k := found(NORM_SLOTS, q)) is not None:
                            h32_tile(n + 1, k)
                    if not has_prev and (k := found(PREP_SLOTS, q - 1)) is not None:
                        w_lo(WSTAGE + k)
                    if q == PAIRS * TILES - 1 and (c := proj_at(q, has_prev, has_next)) is not None:
                        proj_out(n - 1, c)

            over_images(dve, body)
            last_pair = PAIRS * N_IMG - 1
            o_add(last_pair, PAIRS - 1, GRP - 1)
            r_copy(last_pair)
            for c in range(PROJ):
                m, cols = c // 2, slice(c % 2 * HALF, (c % 2 + 1) * HALF)
                dve.wait_ge(proj_done, LAST * PROJ + c + 1)
                dve.wait_ge(last_res_in[m], 16)
                nc.vector.scalar_tensor_tensor(out=last_res(m)[:, cols], in0=last_bank(c), scalar=b_p[:, m:m + 1],
                                               in1=last_res(m)[:, cols], op0=ALU.add, op1=ALU.add).then_inc(res_done, 1)

        @block.gpsimd
        def _(pool):
            def h_lo_tile(m, k):
                pool.wait_ge(h_hi_done, m * KT + k + 1)
                nc.gpsimd.tensor_tensor(h_lo[:, k, :], x_home(k), h_hi[:, k, :].bitcast(fp32),
                                        ALU.subtract).then_inc(h_lo_done, 1)
                pool.wait_ge(h_lo_done, m * KT + k + 1)

            def split_kq(P, par, c, computed=None):
                t, half = c // 2, c % 2
                cols = slice(half * HALF, (half + 1) * HALF)
                pool.wait_ge(qkv32_done, P * CHUNKS + c + 1 if computed is None else computed)
                rows = (slice(0, D), slice(D, P128))
                hi = [Q[rows[hd], par, hd, cols] if t == 2 else K[rows[hd], par, hd, 0, cols] for hd in range(2)]
                count = P * 4 + (c if c < 2 else c - 2) + 1
                for hd in range(2):
                    ins = nc.gpsimd.tensor_tensor(hi[hd], kq32[rows[hd], half, :], one[rows[hd], :].broadcast_to((D, HALF)),
                                                  ALU.mult)
                ins.then_inc(kq_hi_done, 1)
                pool.wait_ge(kq_hi_done, count)
                for hd in range(2):
                    lo = kq32[rows[hd], half, :] if t == 2 else K[rows[hd], par, hd, 1, cols]
                    ins = nc.gpsimd.tensor_tensor(lo, kq32[rows[hd], half, :], hi[hd].bitcast(fp32), ALU.subtract)
                ins.then_inc(split_done, 1)
                pool.wait_ge(split_done, count)

            def divide_pair(P, p):
                pool.wait_ge(r_in, (P + 1) * 32)
                pool.wait_ge(o_add_done, (P + 1) * GRP)
                nc.gpsimd.tensor_tensor(U[:, p, :], U[:, p, :], R[:], ALU.mult).then_inc(mul_done, 1)
                pool.wait_ge(mul_done, P + 1)

            def a_lo_pair(P, p):
                pool.wait_ge(a_hi_done, P + 1)
                nc.gpsimd.tensor_tensor(a_lo[:, p, :], U[:, p, :], a_hi[:, p, :].bitcast(fp32),
                                        ALU.subtract).then_inc(a_lo_done, 1)
                pool.wait_ge(a_lo_done, P + 1)

            def root(m):
                pool.wait_ge(gn_read, 2 * m + 2)
                nc.gpsimd.tensor_tensor(grs[:], gvar[:], m_half[:], ALU.pow).then_inc(root_done, 1)
                pool.wait_ge(root_done, m + 1)

            nc.gpsimd.memset(one[:], 1.0)
            nc.gpsimd.memset(m_half[:], -0.5).then_inc(half_set, 1)
            pool.wait_ge(half_set, 1)
            root(0)
            pool.wait_ge(split_done, 2)
            for c in (4, 5):
                split_kq(0, 0, c, FIRST.index(c) + 1)

            def body(n, has_prev, has_next):
                for q in range(PAIRS * TILES):
                    p, i = q // TILES, q % TILES
                    P = n * PAIRS + p
                    if has_next and (k := found(H_SLOTS, q)) is not None:
                        h_lo_tile(n + 1, k)
                    if (j := qkv_at(q - 1, has_next)) is not None and j[1] not in (2, 3):
                        split_kq(n * PAIRS + j[0], j[0] % 2, j[1])
                    if i == 4 and (p > 0 or has_prev):
                        divide_pair(P - 1, (p - 1) % PAIRS)
                    if (j := a_hi_at(q, has_prev, has_next)) is not None:
                        a_lo_pair(n * PAIRS + j, j % PAIRS)
                    if has_next and q == GN_VAR_SLOT + 1:
                        root(n + 1)

            over_images(pool, body)
            divide_pair(PAIRS * N_IMG - 1, PAIRS - 1)
            a_lo_pair(PAIRS * N_IMG - 1, PAIRS - 1)


def kernel(x, L0_conv_norm_w, L0_conv_norm_b, L0_conv_qkv_w, L0_conv_qkv_b, L0_conv_proj_w, L0_conv_proj_b):
    import numpy as np
    import concourse.bacc as bacc
    from concourse.bass_utils import run_bass_kernel_spmd

    x, nw, nb, qw, qb, pw, pb = (np.asarray(a) for a in (
        x, L0_conv_norm_w, L0_conv_norm_b, L0_conv_qkv_w, L0_conv_qkv_b, L0_conv_proj_w, L0_conv_proj_b))
    group = C // 32
    arrays = {
        "x": np.ascontiguousarray(x.reshape(N_IMG, C, S)),
        "wqkvT": np.ascontiguousarray(qw.T),
        "bqkv": np.ascontiguousarray(qb.reshape(3, PAIRS, P128).transpose(2, 1, 0).reshape(P128, 3 * PAIRS)),
        "wpT": np.ascontiguousarray(pw.T),
        "bp": np.ascontiguousarray(pb.reshape(KT, P128).T),
        "gnw": np.ascontiguousarray(nw.reshape(KT, P128).T),
        "gnb": np.ascontiguousarray(nb.reshape(KT, P128).T),
        "ident_in": np.eye(P128, dtype=np.float32),
        "avg_in": np.kron(np.eye(P128 // group, dtype=np.float32), np.full((group, group), 1.0 / group, np.float32)),
    }
    nc = bacc.Bacc("TRN2", target_bir_lowering=False, num_devices=1, dynamic_dma_scratch_size=1024)
    aps = [nc.dram_tensor(n, a.shape, mybir.dt.from_np(a.dtype), kind="ExternalInput").ap() for n, a in arrays.items()]
    out = nc.dram_tensor("out", (N_IMG, C, S), mybir.dt.float32, kind="ExternalOutput").ap()
    build(nc, *aps, out)
    r = run_bass_kernel_spmd(nc, [arrays], core_ids=[0])
    return r.results[0]["out"].reshape(N_IMG, C, 32, 32)
```
